# Optimizing a Trainium2 kernel written in Bass

```python
import numpy as np
import jax
import jax.numpy as jnp

def _softmax(x, axis=-1):
    return jax.nn.softmax(x, axis=axis)

def _gelu(x):
    return jax.nn.gelu(x, approximate=True)

def _silu(x):
    return jax.nn.silu(x)

def _sigmoid(x):
    return jax.nn.sigmoid(x)

def _layernorm(x, axis=-1, eps=1e-05):
    m = jnp.mean(x, axis=axis, keepdims=True)
    v = jnp.var(x, axis=axis, keepdims=True)
    return (x - m) / jnp.sqrt(v + eps)

def _scatter_add(tgt, idx, src, axis=0):
    return tgt.at[idx].add(src)

def _segment_sum(src, seg, n):
    return jax.ops.segment_sum(src, seg, n)
kernel_name = 'mk_recurrent_d1_jaxref_r8_cbadb0'

def setup_inputs(seed: int=0):
    np.random.seed(seed)
    _w = jnp.asarray

    def _L0_attn_setup():
        import jax, jax.numpy as jnp
        import numpy as np
        import math
        D_MODEL = 128
        D_QUERY = 64
        key = jax.random.key(seed)
        k1, k2, k3, k4 = jax.random.split(key, 4)
        X = jax.random.normal(k1, (4, 512, D_MODEL), dtype=jnp.float32)
        Wq = jax.random.normal(k2, (D_MODEL, D_QUERY), dtype=jnp.float32) * (1.0 / math.sqrt(D_MODEL))
        Wk = jax.random.normal(k3, (D_MODEL, D_QUERY), dtype=jnp.float32) * (1.0 / math.sqrt(D_MODEL))
        Wv = jax.random.normal(k4, (D_MODEL, D_MODEL), dtype=jnp.float32) * (1.0 / math.sqrt(D_MODEL))
        return {'X': X, 'Wq': Wq, 'Wk': Wk, 'Wv': Wv}
    _L0_attn_in = _L0_attn_setup()

    def _L0_ffn_setup():
        import jax, jax.numpy as jnp
        import numpy as np
        D = 128
        H = 512
        E = 8
        B, N = (2, 256)
        key = jax.random.key(seed)
        ks = jax.random.split(key, 5)
        x = jax.random.normal(ks[0], (B, N, D), dtype=jnp.float32)
        W1 = jax.random.normal(ks[1], (E, D, H), dtype=jnp.float32) / np.sqrt(D)
        W2 = jax.random.normal(ks[2], (E, H, D), dtype=jnp.float32) / np.sqrt(H)
        Wg = jax.random.normal(ks[3], (D, E), dtype=jnp.float32) / np.sqrt(D)
        bg = jax.random.normal(ks[4], (E,), dtype=jnp.float32) * 0.01
        return {'x': x, 'W1': W1, 'W2': W2, 'Wg': Wg, 'bg': bg}
    _L0_ffn_in = _L0_ffn_setup()
    _d = {'L0_attn_X': _L0_attn_in['X'], 'L0_attn_Wq': _L0_attn_in['Wq'], 'L0_attn_Wk': _L0_attn_in['Wk'], 'L0_attn_Wv': _L0_attn_in['Wv'], 'L0_ffn_W1': _L0_ffn_in['W1'], 'L0_ffn_W2': _L0_ffn_in['W2'], 'L0_ffn_Wg': _L0_ffn_in['Wg'], 'L0_ffn_bg': _L0_ffn_in['bg']}
    _x0 = _d['L0_attn_X']
    _d['L0_attn_X'] = jax.random.normal(jax.random.fold_in(jax.random.key(seed), 1), (32, 256, 128), dtype=_x0.dtype)
    del _x0
    return _d

def reference(L0_attn_X, L0_attn_Wq, L0_attn_Wk, L0_attn_Wv, L0_ffn_W1, L0_ffn_W2, L0_ffn_Wg, L0_ffn_bg):

    def _L0_attn_ref(X, Wq, Wk, Wv):
        import jax, jax.numpy as jnp
        import numpy as np
        import math
        D_MODEL = 128
        D_QUERY = 64
        B, T, _ = X.shape
        Q = X @ Wq
        K = X @ Wk
        V = X @ Wv
        scores = jnp.einsum('btd,bsd->bts', Q, K)
        causal = jnp.tril(jnp.ones((T, T), dtype=bool))
        scores = jnp.where(causal[None, :, :], scores, -jnp.inf)
        attn = jax.nn.softmax(scores / math.sqrt(D_QUERY), axis=2)
        return attn @ V

    def _L0_ffn_ref(x, W1, W2, Wg, bg):
        import jax, jax.numpy as jnp
        import numpy as np
        D = 128
        H = 512
        E = 8
        B, N = (2, 256)
        b, n, d = x.shape
        e = Wg.shape[1]
        xf = x.reshape(b * n, d)
        logits = xf @ Wg + bg
        one_hot = jax.nn.one_hot(jnp.argmax(logits, axis=-1), e, dtype=x.dtype)
        h = jax.nn.gelu(jnp.einsum('td,edh->eth', xf, W1), approximate=True)
        y = jnp.einsum('eth,ehd->etd', h, W2)
        out = jnp.einsum('etd,te->td', y, one_hot)
        return out.reshape(b, n, d)
    x = L0_attn_X
    xn = _layernorm(x, axis=-1)
    s = _L0_attn_ref(xn, L0_attn_Wq, L0_attn_Wk, L0_attn_Wv)
    g = _silu(_L0_ffn_ref(xn, L0_ffn_W1, L0_ffn_W2, L0_ffn_Wg, L0_ffn_bg))
    x = x + s * g
    return x

_drawn_inputs = setup_inputs


def setup_inputs(seed=0):
    import zlib

    import numpy as np

    out = dict(_drawn_inputs(seed))
    spreads = {}
    factors = {'L0_ffn_bg': 6.415}
    for name, (base, spread) in spreads.items():
        noise = np.random.default_rng([zlib.crc32(name.encode()), seed]).standard_normal(out[name].shape)
        drawn = base * np.exp(spread * noise) if base else spread * noise
        out[name] = jnp.asarray(drawn.astype(out[name].dtype))
    for name, factor in factors.items():
        out[name] = (out[name] * factor).astype(out[name].dtype)
    return out
```

```python
from contextlib import ExitStack

import concourse.bass as bass
from concourse import mybir

P = 128
ALU = mybir.AluOpType
ACT = mybir.ActivationFunctionType
F32 = mybir.dt.float32
F16 = mybir.dt.float16
I32 = mybir.dt.int32
AX = mybir.AxisListType
EPS = 1e-5
BIG = 3.0e38
XN_SCALE = 1024.0
W_TOP = 16384.0


def pipeline(eng, count, unroll, warm, stages):
    last = count + max(lag for lag, _ in stages)
    lo = -(-warm // unroll) * unroll
    turns = max(0, (count - lo) // unroll)
    hi = lo + turns * unroll

    def peeled(s):
        for lag, step in stages:
            k = s - lag
            if 0 <= k < count:
                step(k, k // unroll, k % unroll, k)

    for s in range(min(lo, last) if turns else last):
        peeled(s)
    if turns:
        with eng.Fori(0, turns) as t:
            for j in range(unroll):
                for lag, step in stages:
                    k = lo + j - lag
                    step(t * unroll + k, t + k // unroll, k % unroll, k)
        for s in range(hi, last):
            peeled(s)


def routed_block(nc, X, Wq, Wk, Wv, W1, W2, Wg, bg, out):
    B, T, D = X.shape
    DQ = Wq.shape[1]
    E, _, H = W1.shape
    TOKENS = B * T
    NT = TOKENS // P
    TB = T // P
    GROUP = 4
    NG = NT // GROUP
    HC = H // P
    SLOTS = NT + E - 1
    NPAD = SLOTS - NT
    ROW = 3 * D + 1
    VW = D + E
    assert D == P and TB == 2 and H == 4 * P

    x_tiles = X.rearrange("b (h p) d -> p (b h) d", p=P)
    out_rows = out.rearrange("b t d -> (b t) d")
    w1_dram = W1.rearrange("e d h -> d e h")
    w2_dram = W2.rearrange("e (c p) d -> p (e c) d", p=P)
    bg_row = bg.rearrange("(o e) -> o e", o=1)
    buf = nc.dram_tensor("sorted_rows", (SLOTS * P, ROW), F32, kind="Internal").ap()

    ctx = ExitStack()
    with ctx:
        def sb(name, shape, dt=F32):
            return ctx.enter_context(nc.sbuf_tensor(name, shape, dt))

        def sem(name):
            return ctx.enter_context(nc.semaphore(name))

        x_all = sb("x_all", [P, NT * D])
        xn_all = sb("xn_all", [P, NT * D])
        xnT_all = sb("xnT_all", [P, NT * P])
        v_all = sb("v_all", [P, NT * VW])
        w1_all = sb("w1_all", [P, E * H])
        w1_hi = sb("w1_hi", [P, E * H], F16)
        w1_lo = sb("w1_lo", [P, E * H], F16)
        w2_all = sb("w2_all", [P, E * H])
        wvg = sb("wvg", [P, VW])
        wq_sb = sb("wq_sb", [P, DQ])
        wk_sb = sb("wk_sb", [P, DQ])
        wqT = sb("wqT", [DQ, P])
        wkT = sb("wkT", [DQ, P])
        a_sb = sb("a_sb", [P, P])
        bg_sb = sb("bg_sb", [P, E])
        ident = sb("ident", [P, P])
        mask = sb("mask", [P, 2 * P])
        stats = sb("stats", [P, 2, GROUP, 6])
        moments = sb("moments", [P, 4, GROUP, 2])
        var_eps = sb("var_eps", [P, 4, GROUP])
        rstd = sb("rstd", [P, 4, GROUP])
        neg_half = sb("neg_half", [P, GROUP])
        xn_ring = sb("xn_ring", [P, 2, GROUP * D])
        xnT_ring = sb("xnT_ring", [P, 2, GROUP * P])
        logits = xn_ring[:, 0, 0:NT * E]
        taken = [0]

        def in_x_all(*shape):
            size = 1
            for n in shape:
                size *= n
            view = x_all[:, taken[0]:taken[0] + size]
            taken[0] += size
            if len(shape) == 2:
                return view.rearrange("p (a b) -> p a b", a=shape[0])
            return view

        first_key = sb("first_key", [P, E])
        best = sb("best", [P, NT])
        is_best = in_x_all(NT, E)
        chosen = in_x_all(E, NT)
        running = in_x_all(E, NT)
        zeros = sb("zeros", [P, E * NT])
        row_tot = sb("row_tot", [P, E])
        before = sb("before", [P, E])
        below = sb("below", [P, P])
        ones = sb("ones", [P, P])
        total = sb("total", [P, E])
        total_i = sb("total_i", [P, E], I32)
        tiles_i = sb("tiles_i", [P, E], I32)
        tiles = sb("tiles", [P, E])
        tiles_end = sb("tiles_end", [P, E])
        base = sb("base", [P, E])
        cum_total = sb("cum_total", [P, E])
        pads_before = sb("pads_before", [P, E])
        offset = sb("offset", [P, E])
        pos_f = sb("pos_f", [P, NT])
        ids = sb("ids", [P, NT, 2], I32)
        tile_no = sb("tile_no", [P, SLOTS + 2])
        tile_ge = in_x_all(SLOTS + 2, E)
        expert = sb("expert", [P, SLOTS + 2])
        experts_i = sb("experts_i", [P, SLOTS + 1], I32)
        pad_no = sb("pad_no", [P, NPAD])
        pad_ge = sb("pad_ge", [P, NPAD, E])
        pad_f = sb("pad_f", [P, NPAD])
        pad_i = sb("pad_i", [P, NPAD], I32)
        pad_row = sb("pad_row", [P, ROW])
        w_sum = sb("w_sum", [P, 1])
        w_top = sb("w_top", [P, 1])
        w_pow = sb("w_pow", [P, 1])
        w_recip = sb("w_recip", [P, 1])
        w_scale = sb("w_scale", [P, 1])
        h_scale = sb("h_scale", [P, 1])
        RB = 4
        y_sb = sb("y_sb", [P, 2, T])
        masked = in_x_all(2, 3 * P)
        neg_max = sb("neg_max", [P, 2, TB])
        probs = sb("probs", [P, 2, 3 * P])
        prob_sum = sb("prob_sum", [P, 4, TB])
        inv_sum = sb("inv_sum", [P, 2, TB])
        probsT = sb("probsT", [P, 2, 3 * P])
        rows = in_x_all(RB * TB, ROW + 1)
        taken[0] = 0
        RC = 8
        tile_in = in_x_all(RC, ROW)
        xs_hi = sb("xs_hi", [P, 2, P], F16)
        xs_lo = sb("xs_lo", [P, 2, P], F16)
        hidden = in_x_all(2, H)
        tanh_y = in_x_all(2, D)
        y_gate = in_x_all(2, D)
        y_att = in_x_all(2, D)
        tile_out = in_x_all(RC, D)

        bank = [ctx.enter_context(nc.psum_tensor(f"bank{i}", [P, 512], F32)) for i in range(8)]

        w_loaded = sem("w_loaded")
        w1_loaded = sem("w1_loaded")
        w2_loaded = sem("w2_loaded")
        x_loaded = [sem(f"x_loaded{i}") for i in range(4)]
        const_step = sem("const_step")
        consts_ready = sem("consts_ready")
        wT_done = sem("wT_done")
        wT_copied = sem("wT_copied")
        a_done = sem("a_done")
        a_ready = sem("a_ready")
        stats_done = sem("stats_done")
        moments_ready = sem("moments_ready")
        eps_added = sem("eps_added")
        rstd_ready = sem("rstd_ready")
        xn_ready = sem("xn_ready")
        xn_stored = [sem(f"xn_stored{i}") for i in range(2)]
        xnT_done = sem("xnT_done")
        xnT_ready = sem("xnT_ready")
        xnT_stored = sem("xnT_stored")
        v_done = sem("v_done")
        v_ready = sem("v_ready")
        route_step = sem("route_step")
        counts_in = sem("counts_in")
        counts_done = sem("counts_done")
        places_ready = sem("places_ready")
        experts_ready = sem("experts_ready")
        pads_ready = sem("pads_ready")
        w_summed = sem("w_summed")
        scale_ready = sem("scale_ready")
        w_split = sem("w_split")
        hi_ready = sem("hi_ready")
        y_done = sem("y_done")
        y_ready = sem("y_ready")
        scores_done = sem("scores_done")
        masked_ready = sem("masked_ready")
        probs_ready = sem("probs_ready")
        probsT_done = sem("probsT_done")
        probsT_ready = sem("probsT_ready")
        att_done = sem("att_done")
        inv_ready = sem("inv_ready")
        row_x = [sem(f"row_x{i}") for i in range(RB)]
        row_xn = sem("row_xn")
        row_ids = sem("row_ids")
        row_att = sem("row_att")
        row_sent = [sem(f"row_sent{i}") for i in range(RB)]
        pads_sent = sem("pads_sent")
        in_loaded = [sem(f"in_loaded{i}") for i in range(RC)]
        xsT_done = sem("xsT_done")
        xs_hi_ready = sem("xs_hi_ready")
        xs_lo_ready = sem("xs_lo_ready")
        up_done = sem("up_done")
        hidden_ready = sem("hidden_ready")
        down_done = sem("down_done")
        tanh_ready = sem("tanh_ready")
        gate_ready = sem("gate_ready")
        gated_ready = sem("gated_ready")
        out_ready = sem("out_ready")
        out_sent = [sem(f"out_sent{i}") for i in range(RC)]

        def steady(eng, *waits):
            counts = [n if isinstance(n, int) else eng.to_reg(n) for _, n in waits]
            eng.wait_ge(consts_ready, 3)
            for (s, _), n in zip(waits, counts):
                eng.wait_ge(s, n)

        block = ctx.enter_context(nc.Block())

        @block.sync
        def _(sp):
            def load_x(g, turn, slot, least):
                if least >= 4:
                    sp.wait_ge(x_loaded[slot], 16 * turn)
                sp.dma_start(x_all[:, bass.ds(g * (GROUP * D), GROUP * D)],
                             x_tiles[:, bass.ds(g * GROUP, GROUP), :]).then_inc(x_loaded[slot], 16)

            def load_row_x(i, turn, slot, least):
                if least >= RB:
                    sp.wait_ge(row_sent[slot], 16 * TB * turn)
                sp.dma_start(rows[:, slot * TB:(slot + 1) * TB, 0:D],
                             x_tiles[:, bass.ds(i * TB, TB), :]).then_inc(row_x[slot], 16)

            def load_tile(k, turn, slot, least):
                if least >= RC:
                    sp.wait_ge(out_sent[slot], 16 * turn)
                sp.dma_start(tile_in[:, slot, :], buf[bass.ds(k * P, P), :]).then_inc(in_loaded[slot], 16)

            def load_rest(g, turn, slot, least):
                if least >= 2:
                    load_x(g, turn, slot, least)

            for g in range(2):
                load_x(g, 0, g, 0)
            sp.dma_start(wvg[:, 0:D], Wv).then_inc(w_loaded, 16)
            sp.dma_start(wvg[:, D:VW], Wg).then_inc(w_loaded, 16)
            sp.dma_start(wq_sb[:, :], Wq).then_inc(w_loaded, 16)
            sp.dma_start(wk_sb[:, :], Wk).then_inc(w_loaded, 16)
            sp.dma_start(bg_sb[:, :], bg_row.partition_broadcast(P)).then_inc(w_loaded, 16)
            pipeline(sp, NG, 4, 4, [(0, load_rest)])
            sp.dma_start(w1_all[:, :].rearrange("p (e h) -> p e h", e=E), w1_dram).then_inc(w1_loaded, 16)
            sp.dma_start(w2_all[:, :].rearrange("p (c d) -> p c d", d=D), w2_dram).then_inc(w2_loaded, 16)
            sp.wait_ge(xn_ready, NG)
            pipeline(sp, B, RB, RB, [(0, load_row_x)])
            sp.wait_ge(pads_sent, 16 * NPAD)
            for slot in range(RB):
                sp.wait_ge(row_sent[slot], 16 * TB * (B // RB))
            pipeline(sp, SLOTS, RC, RC, [(0, load_tile)])
            for slot in range(RC):
                sp.wait_ge(out_sent[slot], 16 * len(range(slot, SLOTS, RC)))

        @block.gpsimd
        def _(pool):
            pool.memset(neg_half[:, :], -0.5)
            pool.memset(ones[:, :], 1.0)
            pool.memset(ident[:, :], 0.0).then_inc(const_step, 1)
            pool.memset(mask[:, :], 0.0).then_inc(const_step, 1)
            pool.memset(below[:, :], 1.0).then_inc(const_step, 1)
            pool.wait_ge(const_step, 3)
            pool.affine_select(out=ident[:, :], in_=ident[:, :], compare_op=ALU.not_equal, fill=1.0,
                               base=0, pattern=[[-1, P]], channel_multiplier=1).then_inc(consts_ready, 1)
            pool.affine_select(out=mask[:, P:2 * P], in_=mask[:, P:2 * P], compare_op=ALU.is_ge, fill=-BIG,
                               base=0, pattern=[[-1, P]], channel_multiplier=1).then_inc(consts_ready, 1)
            pool.affine_select(out=below[:, :], in_=below[:, :], compare_op=ALU.is_gt, fill=0.0,
                               base=0, pattern=[[1, P]], channel_multiplier=-1).then_inc(consts_ready, 1)

            pool.iota(ids[:, :, 0], pattern=[[P, NT]], base=0, channel_multiplier=1).then_inc(consts_ready, 1)
            pool.memset(zeros[:, :], 0.0)
            pool.memset(pad_row[:, 0:3 * D], 0.0)
            pool.memset(pad_row[:, 3 * D:ROW].bitcast(I32), TOKENS)
            for e in range(E):
                pool.memset(first_key[:, e:e + 1], float(E - e))
            pool.iota(pad_no[:, :], pattern=[[P, NPAD]], base=0, channel_multiplier=1,
                      allow_small_or_imprecise_dtypes=True)
            pool.iota(tile_no[:, :], pattern=[[1, SLOTS + 2]], base=-1, channel_multiplier=0,
                      allow_small_or_imprecise_dtypes=True).then_inc(consts_ready, 1)

            def rstd_of(g, turn, slot, least):
                steady(pool, (moments_ready, g + 1))
                pool.tensor_scalar(var_eps[:, slot, :], moments[:, slot, :, 1], EPS, None,
                                   ALU.add).then_inc(eps_added, 1)
                pool.wait_ge(eps_added, g + 1)
                pool.tensor_tensor(rstd[:, slot, :], var_eps[:, slot, :], neg_half[:, :],
                                   ALU.pow).then_inc(rstd_ready, 1)

            pool.wait_ge(consts_ready, 3)
            pipeline(pool, NG, 4, 4, [(0, rstd_of)])
            pool.wait_ge(pads_ready, 1)
            for m in range(NPAD):
                pool.indirect_dma_start(out=buf[:, :], in_=pad_row[:, :], in_offset=None,
                                        out_offset=bass.IndirectOffsetOnAxis(ap=pad_i[:, m:m + 1], axis=0),
                                        bounds_check=SLOTS * P - 1,
                                        oob_is_err=False).then_inc(pads_sent, 16)

            def send(i, turn, slot, least):
                steady(pool, (row_x[slot], 16 * (turn + 1)), (row_xn, i + 1), (row_ids, i + 1),
                       (row_att, i + 1))
                for h in range(TB):
                    r = rows[:, slot * TB + h, :]
                    pool.indirect_dma_start(
                        out=buf[:, :], in_=r[:, 0:ROW], in_offset=None,
                        out_offset=bass.IndirectOffsetOnAxis(ap=r[:, ROW:ROW + 1].bitcast(I32), axis=0),
                        bounds_check=SLOTS * P - 1, oob_is_err=False).then_inc(row_sent[slot], 16)

            pipeline(pool, B, RB, RB, [(0, send)])

            def send_out(k, turn, slot, least):
                steady(pool, (out_ready, k + 1))
                pool.indirect_dma_start(
                    out=out_rows, in_=tile_out[:, slot, :], in_offset=None,
                    out_offset=bass.IndirectOffsetOnAxis(
                        ap=tile_in[:, slot, 3 * D:ROW].bitcast(I32), axis=0),
                    bounds_check=TOKENS - 1, oob_is_err=False).then_inc(out_sent[slot], 16)

            pipeline(pool, SLOTS, RC, RC, [(0, send_out)])

        @block.scalar
        def _(act):
            act.wait_ge(wT_done, 2)
            act.copy(wqT[:, :], bank[7][0:DQ, 0:P]).then_inc(wT_copied, 1)
            act.copy(wkT[:, :], bank[7][0:DQ, P:2 * P]).then_inc(wT_copied, 1)
            act.wait_ge(a_done, 1)
            act.copy(a_sb[:, :], bank[7][:, 2 * P:3 * P]).then_inc(a_ready, 1)

            def xnT_out(g, turn, slot, least):
                act.wait_ge(xnT_done, g + 1)
                if least >= 2:
                    act.wait_ge(v_done, g - 1)
                act.copy(xnT_ring[:, slot % 2, :], bank[slot % 2][:, :]).then_inc(xnT_ready, 1)
                act.copy(xnT_all[:, bass.ds(g * (GROUP * P), GROUP * P)],
                         bank[slot % 2][:, :]).then_inc(xnT_stored, 1)
                act.wait_ge(xn_ready, g + 1)
                act.dma_start(xn_all[:, bass.ds(g * (GROUP * D), GROUP * D)],
                              xn_ring[:, slot % 2, :]).then_inc(xn_stored[slot % 2], 16)

            def v_out(g, turn, slot, least):
                act.wait_ge(v_done, g + 1)
                for h in range(2):
                    last = act.copy(v_all[:, bass.ds(g * (GROUP * VW) + h * 2 * VW, 2 * VW)],
                                    bank[2 + 2 * (slot % 2) + h][:, 0:2 * VW])
                last.then_inc(v_ready, 1)

            pipeline(act, NG, 4, 4, [(0, xnT_out), (1, v_out)])
            act.wait_ge(w1_loaded, 16)
            act.activation(w1_lo[:, :], w1_all[:, :], ACT.Abs, accum_out=w_sum[:, 0:1]).then_inc(w_summed, 1)
            act.wait_ge(scale_ready, 1)

            def y_out(i, turn, slot, least):
                act.wait_ge(y_done, i + 1)
                if least >= 2:
                    act.wait_ge(scores_done, i - 1)
                act.copy(y_sb[:, slot % 2, :],
                         bank[6 + slot % 2][:, 0:T]).then_inc(y_ready, 1)

            def softmax(i, turn, slot, least):
                s = slot % 2
                act.wait_ge(masked_ready, i + 1)
                if least >= 2:
                    act.wait_ge(probsT_done, i - 1)
                if least >= 4:
                    act.wait_ge(inv_ready, i - 3)
                act.activation(probs[:, s, 0:P], masked[:, s, 0:P], ACT.Exp, bias=neg_max[:, s, 0:1],
                               scale=-1.0, accum_out=prob_sum[:, slot, 0:1])
                act.activation(probs[:, s, P:3 * P], masked[:, s, P:3 * P], ACT.Exp, bias=neg_max[:, s, 1:2],
                               scale=-1.0, accum_out=prob_sum[:, slot, 1:2]).then_inc(probs_ready, 1)

            def rest(i, turn, slot, least):
                if least >= RB:
                    act.wait_ge(row_sent[slot], 16 * TB * turn)
                act.copy(rows[:, slot * TB:(slot + 1) * TB, D:2 * D],
                         xn_all[:, bass.ds(i * (TB * D), TB * D)].rearrange("p (n d) -> p n d", d=D)
                         ).then_inc(row_xn, 1)
                act.activation(w1_hi[:, bass.ds(i * P, P)], w1_all[:, bass.ds(i * P, P)], ACT.Copy,
                               scale=w_scale[:, 0:1]).then_inc(hi_ready, 1)

            pipeline(act, B, 4, 8, [(0, y_out), (1, softmax), (2, rest)])

            def gelu(k, turn, slot, least):
                s = slot % 2
                act.wait_ge(up_done, k + 1)
                if least >= 2:
                    act.wait_ge(down_done, k - 1)
                act.activation(hidden[:, s, :], bank[s][:, :], ACT.Gelu_apprx_tanh,
                               scale=h_scale[:, 0:1]).then_inc(hidden_ready, 1)

            def tanh(k, turn, slot, least):
                s = slot % 2
                act.wait_ge(down_done, k + 1)
                if least >= 2:
                    act.wait_ge(gate_ready, k - 1)
                act.activation(tanh_y[:, s, :], bank[2 + s][:, 0:D], ACT.Tanh,
                               scale=0.5).then_inc(tanh_ready, 1)

            pipeline(act, SLOTS, 4, 4, [(0, gelu), (1, tanh)])

        @block.vector
        def _(dve):
            def stats_of(g, turn, slot, least):
                dve.wait_ge(x_loaded[slot], 16 * (turn + 1))
                if least >= 2:
                    dve.wait_ge(moments_ready, g - 1)
                for j in range(GROUP):
                    last = dve.bn_stats(stats[:, slot % 2, j, :],
                                        x_all[:, bass.ds(g * (GROUP * D) + j * D, D)])
                last.then_inc(stats_done, 1)
                if least >= 4:
                    dve.wait_ge(xn_ready, g - 3)
                    dve.wait_ge(eps_added, g - 3)
                steady(dve, (stats_done, g + 1))
                for j in range(GROUP):
                    last = dve.bn_aggr(moments[:, slot, j, :], stats[:, slot % 2, j, :])
                last.then_inc(moments_ready, 1)

            def normalise(g, turn, slot, least):
                dve.wait_ge(rstd_ready, g + 1)
                dve.wait_ge(moments_ready, g + 1)
                if least >= 2:
                    dve.wait_ge(xnT_done, g - 1)
                    dve.wait_ge(xn_stored[slot % 2], 8 * (g - slot % 2))
                for j in range(GROUP):
                    last = dve.tensor_scalar(xn_ring[:, slot % 2, j * D:(j + 1) * D],
                                             x_all[:, bass.ds(g * (GROUP * D) + j * D, D)],
                                             moments[:, slot, j, 0:1], rstd[:, slot, j:j + 1],
                                             ALU.subtract, ALU.mult)
                last.then_inc(xn_ready, 1)

            dve.wait_ge(consts_ready, 3)
            pipeline(dve, NG, 4, 4, [(0, stats_of), (1, normalise)])

            steps = [0]

            def then(ins):
                steps[0] += 1
                ins.then_inc(route_step, 1)
                dve.wait_ge(route_step, steps[0])

            lg = logits.rearrange("p (n e) -> p n e", e=E)
            chosen_flat = chosen[:, :, :].rearrange("p e n -> p (e n)")
            running_flat = running[:, :, :].rearrange("p e n -> p (e n)")
            by_tile = chosen[:, :, :].rearrange("p e n -> p n e")
            run_by_tile = running[:, :, :].rearrange("p e n -> p n e")
            dve.wait_ge(v_ready, NG)
            dve.wait_ge(xn_stored[0], 16 * NG // 2)
            dve.wait_ge(xn_stored[1], 16 * NG // 2)
            dve.wait_ge(consts_ready, 5)
            dve.wait_ge(w_loaded, 80)
            then(dve.tensor_tensor(lg, v_all[:, :].rearrange("p (n v) -> p n v", v=VW)[:, :, D:VW],
                                   bg_sb[:, None, :].broadcast_to([P, NT, E]), ALU.add))
            then(dve.tensor_reduce(best[:, :], lg, AX.X, ALU.max))
            then(dve.tensor_tensor(is_best[:, :, :], lg, best[:, :, None].broadcast_to([P, NT, E]), ALU.is_ge))
            then(dve.tensor_tensor(is_best[:, :, :], is_best[:, :, :],
                                   first_key[:, None, :].broadcast_to([P, NT, E]), ALU.mult))
            then(dve.tensor_reduce(best[:, :], is_best[:, :, :], AX.X, ALU.max))
            then(dve.tensor_tensor(by_tile, first_key[:, None, :].broadcast_to([P, NT, E]),
                                   best[:, :, None].broadcast_to([P, NT, E]), ALU.is_equal))
            then(dve.tensor_tensor_scan(running_flat, zeros[:, :], chosen_flat, 0.0, ALU.add, ALU.add))
            dve.memset(before[:, 0:1], 0.0)
            then(dve.tensor_copy(before[:, 1:E], running[:, 0:E - 1, NT - 1]))
            then(dve.tensor_tensor(row_tot[:, :], running[:, :, NT - 1], before[:, :], ALU.subtract))
            dve.engine_nop().then_inc(counts_in, 1)
            dve.wait_ge(counts_done, 1)
            lower = bank[5][:, 0:E]
            then(dve.tensor_copy(total[:, :], bank[5][:, E:2 * E]))
            then(dve.tensor_scalar(total_i[:, :], total[:, :], float(P - 1), None, ALU.add))
            then(dve.tensor_scalar(tiles_i[:, :], total_i[:, :], 7, None, ALU.arith_shift_right))
            then(dve.tensor_copy(tiles[:, :], tiles_i[:, :]))
            then(dve.tensor_tensor_scan(tiles_end[:, :], zeros[:, 0:E], tiles[:, :], 0.0, ALU.add, ALU.add))
            then(dve.tensor_tensor(base[:, :], tiles_end[:, :], tiles[:, :], ALU.subtract))
            then(dve.tensor_scalar(base[:, :], base[:, :], float(P), None, ALU.mult))
            then(dve.tensor_tensor(offset[:, :], base[:, :], before[:, :], ALU.subtract))
            then(dve.scalar_tensor_tensor(offset[:, :], offset[:, :], -1.0, lower, ALU.add, ALU.add))
            then(dve.tensor_tensor(run_by_tile, run_by_tile, offset[:, None, :].broadcast_to([P, NT, E]), ALU.add))
            then(dve.tensor_tensor(running_flat, running_flat, chosen_flat, ALU.mult))
            then(dve.tensor_reduce(pos_f[:, :], run_by_tile, AX.X, ALU.add))
            dve.tensor_copy(ids[:, :, 1], pos_f[:, :]).then_inc(places_ready, 1)
            then(dve.tensor_tensor_scan(cum_total[:, :], zeros[:, 0:E], total[:, :], 0.0, ALU.add, ALU.add))
            then(dve.tensor_tensor(cum_total[:, :], cum_total[:, :], total[:, :], ALU.subtract))
            then(dve.tensor_tensor(pads_before[:, :], base[:, :], cum_total[:, :], ALU.subtract))
            then(dve.tensor_tensor(pad_ge[:, :, :], pad_no[:, :, None].broadcast_to([P, NPAD, E]),
                                   pads_before[:, None, :].broadcast_to([P, NPAD, E]), ALU.is_ge))
            then(dve.tensor_tensor(pad_ge[:, :, :], pad_ge[:, :, :],
                                   total[:, None, :].broadcast_to([P, NPAD, E]), ALU.mult))
            then(dve.tensor_reduce(pad_f[:, :], pad_ge[:, :, :], AX.X, ALU.add))
            dve.tensor_tensor(pad_i[:, :], pad_f[:, :], pad_no[:, :], ALU.add).then_inc(pads_ready, 1)
            then(dve.tensor_tensor(tile_ge[:, :, :], tile_no[:, :, None].broadcast_to([P, SLOTS + 2, E]),
                                   tiles_end[:, None, :].broadcast_to([P, SLOTS + 2, E]), ALU.is_ge))
            then(dve.tensor_reduce(expert[:, :], tile_ge[:, :, :], AX.X, ALU.add))
            then(dve.tensor_scalar(expert[:, :], expert[:, :], float(E - 1), None, ALU.min))
            dve.scalar_tensor_tensor(experts_i[:, :], expert[:, 1:SLOTS + 2], float(E),
                                     expert[:, 0:SLOTS + 1], ALU.mult, ALU.add).then_inc(experts_ready, 1)
            dve.wait_ge(counts_done, 2)
            then(dve.tensor_reduce(w_top[:, :], bank[4][:, 0:P], AX.X, ALU.max))
            then(dve.tensor_scalar(w_top[:, :], w_top[:, :], 1e-30, None, ALU.max))
            then(dve.tensor_scalar(w_pow[:, :].bitcast(I32), w_top[:, :].bitcast(I32), 0x7F800000, None,
                                   ALU.bitwise_and))
            then(dve.reciprocal(w_recip[:, :], w_pow[:, :]))
            then(dve.tensor_scalar(h_scale[:, :], w_pow[:, :], 1.0 / (W_TOP * XN_SCALE), None, ALU.mult))
            dve.tensor_scalar(w_scale[:, :], w_recip[:, :], W_TOP, None, ALU.mult).then_inc(scale_ready, 1)
            dve.wait_ge(scale_ready, 1)
            dve.wait_ge(places_ready, 1)

            def mask_max(i, turn, slot, least):
                s = slot % 2
                if least >= 2:
                    dve.wait_ge(probs_ready, i - 1)
                steady(dve, (scores_done, i + 1))
                dve.tensor_tensor_reduce(masked[:, s, 0:P], bank[s][:, 0:P], mask[:, P:2 * P],
                                         -(DQ ** -0.5), BIG, ALU.add, ALU.min, neg_max[:, s, 0:1])
                dve.tensor_tensor_reduce(masked[:, s, P:3 * P], bank[s][:, P:3 * P], mask[:, :],
                                         -(DQ ** -0.5), BIG, ALU.add, ALU.min,
                                         neg_max[:, s, 1:2]).then_inc(masked_ready, 1)

            def probsT_out(i, turn, slot, least):
                s = slot % 2
                dve.wait_ge(probsT_done, i + 1)
                if least >= 2:
                    dve.wait_ge(att_done, i - 1)
                dve.tensor_copy(probsT[:, s, :], bank[2 + s][:, 0:3 * P]).then_inc(probsT_ready, 1)

            def att_out(i, turn, slot, least):
                s = slot % 2
                dve.wait_ge(probs_ready, i + 1)
                if least >= 2:
                    dve.wait_ge(row_att, i - 1)
                dve.reciprocal(inv_sum[:, s, :], prob_sum[:, slot, :]).then_inc(inv_ready, 1)
                dve.wait_ge(hi_ready, i + 1)
                dve.scalar_tensor_tensor(w1_lo[:, bass.ds(i * P, P)], w1_all[:, bass.ds(i * P, P)],
                                         w_scale[:, 0:1], w1_hi[:, bass.ds(i * P, P)], ALU.mult,
                                         ALU.subtract).then_inc(w_split, 1)
                if least >= RB:
                    dve.wait_ge(row_sent[slot], 16 * TB * turn)
                r = rows[:, slot * TB:(slot + 1) * TB, :]
                dve.tensor_copy(r[:, :, 3 * D:3 * D + 2].bitcast(I32),
                                ids[:, bass.ds(i * TB, TB), :]).then_inc(row_ids, 1)
                dve.wait_ge(att_done, i + 1)
                dve.wait_ge(inv_ready, i + 1)
                dve.tensor_tensor(r[:, :, 2 * D:3 * D],
                                  bank[4 + s][:, 0:T].rearrange("p (n d) -> p n d", d=D),
                                  inv_sum[:, s, :, None].broadcast_to([P, TB, D]),
                                  ALU.mult).then_inc(row_att, 1)

            pipeline(dve, B, 4, 8, [(0, mask_max), (1, probsT_out), (2, att_out)])

            def split_xs(k, turn, slot, least):
                s = slot % 2
                dve.wait_ge(xsT_done, k + 1)
                if least >= 2:
                    dve.wait_ge(up_done, k - 1)
                xsT = bank[4 + s][:, 0:P]
                dve.tensor_scalar(xs_hi[:, s, :], xsT, XN_SCALE, None, ALU.mult).then_inc(xs_hi_ready, 1)
                dve.wait_ge(xs_hi_ready, k + 1)
                dve.scalar_tensor_tensor(xs_lo[:, s, :], xsT, XN_SCALE, xs_hi[:, s, :], ALU.mult,
                                         ALU.subtract).then_inc(xs_lo_ready, 1)

            def combine(k, turn, slot, least):
                s = slot % 2
                dve.wait_ge(tanh_ready, k + 1)
                if least >= 2:
                    dve.wait_ge(gated_ready, k - 1)
                dve.scalar_tensor_tensor(y_gate[:, s, :], tanh_y[:, s, :], 1.0,
                                         bank[2 + s][:, 0:D], ALU.add,
                                         ALU.mult).then_inc(gate_ready, 1)
                dve.wait_ge(gate_ready, k + 1)
                if least >= 2:
                    dve.wait_ge(out_ready, k - 1)
                dve.tensor_tensor(y_att[:, s, :], y_gate[:, s, :], tile_in[:, slot, 2 * D:3 * D],
                                  ALU.mult).then_inc(gated_ready, 1)
                dve.wait_ge(gated_ready, k + 1)
                if least >= RC:
                    dve.wait_ge(out_sent[slot], 16 * turn)
                dve.scalar_tensor_tensor(tile_out[:, slot, :], y_att[:, s, :], 0.5, tile_in[:, slot, 0:D],
                                         ALU.mult, ALU.add).then_inc(out_ready, 1)

            pipeline(dve, SLOTS, RC, RC + 3, [(0, split_xs), (3, combine)])

        @block.tensor
        def _(pe):
            pe.wait_ge(consts_ready, 3)
            pe.wait_ge(w_loaded, 80)
            pe.transpose(bank[7][0:DQ, 0:P], wq_sb[:, :], ident[:, :]).then_inc(wT_done, 1)
            pe.transpose(bank[7][0:DQ, P:2 * P], wk_sb[:, :], ident[:, :]).then_inc(wT_done, 1)
            pe.wait_ge(wT_copied, 2)
            pe.matmul(bank[7][:, 2 * P:3 * P], wqT[:, :], wkT[:, :], start=True, stop=True).then_inc(a_done, 1)

            def xnT_of(g, turn, slot, least):
                pe.wait_ge(xn_ready, g + 1)
                if least >= 2:
                    pe.wait_ge(xnT_stored, g - 1)
                for j in range(GROUP):
                    last = pe.transpose(bank[slot % 2][:, j * P:(j + 1) * P],
                                        xn_ring[:, slot % 2, j * D:(j + 1) * D], ident[:, :])
                last.then_inc(xnT_done, 1)

            def v_of(g, turn, slot, least):
                pe.wait_ge(xnT_ready, g + 1)
                if least >= 2:
                    pe.wait_ge(v_ready, g - 1)
                for j in range(GROUP):
                    b = bank[2 + 2 * (slot % 2) + j // 2]
                    last = pe.matmul(b[:, (j % 2) * VW:(j % 2 + 1) * VW],
                                     xnT_ring[:, slot % 2, j * P:(j + 1) * P], wvg[:, :],
                                     start=True, stop=True)
                last.then_inc(v_done, 1)

            pipeline(pe, NG, 4, 4, [(0, xnT_of), (1, v_of)])

            pe.wait_ge(a_ready, 1)
            pe.wait_ge(counts_in, 1)
            pe.matmul(bank[5][:, 0:E], below[:, :], row_tot[:, :], start=True, stop=True)
            pe.matmul(bank[5][:, E:2 * E], ones[:, :], row_tot[:, :], start=True,
                      stop=True).then_inc(counts_done, 1)
            pe.wait_ge(w_summed, 1)
            pe.matmul(bank[4][:, 0:P], w_sum[:, 0:1].broadcast_to([P, P]), ident[:, :], start=True,
                      stop=True).then_inc(counts_done, 1)
            pe.wait_ge(v_ready, NG)
            pe.wait_ge(xnT_stored, NG)

            def y_of(i, turn, slot, least):
                if least >= 2:
                    pe.wait_ge(y_ready, i - 1)
                pe.matmul(bank[6 + slot % 2][:, 0:T], a_sb[:, :],
                          xnT_all[:, bass.ds(i * T, T)], start=True, stop=True).then_inc(y_done, 1)

            def scores_of(i, turn, slot, least):
                s = slot % 2
                pe.wait_ge(y_ready, i + 1)
                if least >= 2:
                    pe.wait_ge(masked_ready, i - 1)
                pe.matmul(bank[s][:, 0:P], y_sb[:, s, 0:P], xnT_all[:, bass.ds(i * T, P)],
                          start=True, stop=True)
                pe.matmul(bank[s][:, P:3 * P], y_sb[:, s, P:2 * P], xnT_all[:, bass.ds(i * T, T)],
                          start=True, stop=True).then_inc(scores_done, 1)

            def probsT_of(i, turn, slot, least):
                s = slot % 2
                pe.wait_ge(probs_ready, i + 1)
                if least >= 2:
                    pe.wait_ge(probsT_ready, i - 1)
                for j in range(3):
                    last = pe.transpose(bank[2 + s][:, j * P:(j + 1) * P], probs[:, s, j * P:(j + 1) * P],
                                        ident[:, :])
                last.then_inc(probsT_done, 1)

            def att_of(i, turn, slot, least):
                s = slot % 2
                pe.wait_ge(probsT_ready, i + 1)
                if least >= 2:
                    pe.wait_ge(row_att, i - 1)
                o = bank[4 + s][:, 0:T]
                v0, v1 = (v_all[:, bass.ds(i * (TB * VW) + h * VW, D)] for h in range(TB))
                pe.matmul(o[:, 0:D], probsT[:, s, 0:P], v0, start=True, stop=True)
                pe.matmul(o[:, D:2 * D], probsT[:, s, P:2 * P], v0, start=True, stop=False)
                pe.matmul(o[:, D:2 * D], probsT[:, s, 2 * P:3 * P], v1, start=False,
                          stop=True).then_inc(att_done, 1)

            pipeline(pe, B, 4, 8, [(0, y_of), (1, scores_of), (2, probsT_of), (3, att_of)])

            pe.wait_ge(experts_ready, 1)
            pe.wait_ge(w_split, B)
            pe.wait_ge(w2_loaded, 16)

            def xsT_of(k, turn, slot, least):
                s = slot % 2
                pe.wait_ge(in_loaded[slot], 16 * (turn + 1))
                if least >= 2:
                    pe.wait_ge(xs_lo_ready, k - 1)
                pe.transpose(bank[4 + s][:, 0:P], tile_in[:, slot, D:2 * D],
                             ident[:, :]).then_inc(xsT_done, 1)

            def load_experts(k):
                return nc.values_load(experts_i[0:1, bass.ds(k, 1)], engines=[pe.engine], min_val=0,
                                      max_val=E * E - 1,
                                      skip_runtime_bounds_check_because="each expert is at most E - 1")

            experts = [None]

            def up(k, turn, slot, least):
                experts[0] = load_experts(k)
                own = pe.snap(experts[0] // E * H)
                s = slot % 2
                pe.wait_ge(xs_lo_ready, k + 1)
                if least >= 2:
                    pe.wait_ge(hidden_ready, k - 1)
                for c in range(HC):
                    h = bank[s][:, c * P:(c + 1) * P]
                    hi = w1_hi[:, bass.ds(own + c * P, P)]
                    lo = w1_lo[:, bass.ds(own + c * P, P)]
                    pe.matmul(h, hi, xs_hi[:, s, :], start=True, stop=False)
                    pe.matmul(h, hi, xs_lo[:, s, :], start=False, stop=False)
                    last = pe.matmul(h, lo, xs_hi[:, s, :], start=False, stop=True)
                last.then_inc(up_done, 1)

            def down(k, turn, slot, least):
                if least == SLOTS - 1:
                    experts[0] = load_experts(k + 1)
                own = pe.snap(experts[0] % E * H)
                s = slot % 2
                pe.wait_ge(hidden_ready, k + 1)
                if least >= 2:
                    pe.wait_ge(gate_ready, k - 1)
                for c in range(HC):
                    last = pe.matmul(bank[2 + s][:, 0:D], hidden[:, s, c * P:(c + 1) * P],
                                     w2_all[:, bass.ds(own + c * P, P)], start=(c == 0),
                                     stop=(c == HC - 1))
                last.then_inc(down_done, 1)

            pipeline(pe, SLOTS, RC, 4, [(0, xsT_of), (1, up), (2, down)])


_INS = ['L0_attn_X', 'L0_attn_Wq', 'L0_attn_Wk', 'L0_attn_Wv', 'L0_ffn_W1', 'L0_ffn_W2', 'L0_ffn_Wg', 'L0_ffn_bg']
_OUT = ((32, 256, 128), 'float32')


def kernel(**inputs):
    import numpy as _np
    import concourse.bacc as _bacc
    from concourse import mybir as _mybir
    from concourse.bass_utils import run_bass_kernel_spmd as _run

    nc = _bacc.Bacc("TRN2", target_bir_lowering=False, num_devices=1)
    arrays, args = {}, []
    for name in _INS:
        a = _np.ascontiguousarray(inputs[name])
        arrays[f"in_{name}_dram"] = a
        args.append(nc.dram_tensor(f"in_{name}_dram", a.shape, _mybir.dt.from_np(a.dtype), kind="ExternalInput").ap())
    shape, dtype = _OUT
    args.append(nc.dram_tensor("out_dram", shape, _mybir.dt.from_np(_np.dtype(dtype)), kind="ExternalOutput").ap())
    routed_block(nc, *args)
    r = _run(nc, [arrays], core_ids=[0])
    return r.results[0]["out_dram"]
```

```python
from contextlib import ExitStack

import concourse.bass as bass
from concourse import mybir

P = 128
ALU = mybir.AluOpType
ACT = mybir.ActivationFunctionType
F32 = mybir.dt.float32
F16 = mybir.dt.float16
I32 = mybir.dt.int32
AX = mybir.AxisListType
EPS = 1e-5
BIG = 3.0e38
XN_SCALE = 1024.0
W_TOP = 16384.0


def pipeline(eng, count, unroll, warm, stages):
    last = count + max(lag for lag, _ in stages)
    lo = -(-warm // unroll) * unroll
    turns = max(0, (count - lo) // unroll)
    hi = lo + turns * unroll

    def peeled(s):
        for lag, step in stages:
            k = s - lag
            if 0 <= k < count:
                step(k, k // unroll, k % unroll, k)

    for s in range(min(lo, last) if turns else last):
        peeled(s)
    if turns:
        with eng.Fori(0, turns) as t:
            for j in range(unroll):
                for lag, step in stages:
                    k = lo + j - lag
                    step(t * unroll + k, t + k // unroll, k % unroll, k)
        for s in range(hi, last):
            peeled(s)


def routed_block(nc, X, Wq, Wk, Wv, W1, W2, Wg, bg, out):
    B, T, D = X.shape
    DQ = Wq.shape[1]
    E, _, H = W1.shape
    TOKENS = B * T
    NT = TOKENS // P
    TB = T // P
    GROUP = 4
    NG = NT // GROUP
    HC = H // P
    SLOTS = NT + E
    PAIRS = NT // 2 + E - 1
    VOID = 1 << TOKENS.bit_length()
    NPAD = SLOTS - NT
    ROW = 3 * D + 1
    VW = D + E
    assert D == P and TB == 2 and H == 4 * P

    x_tiles = X.rearrange("b (h p) d -> p (b h) d", p=P)
    out_rows = out.rearrange("b t d -> (b t) d")
    w1_dram = W1.rearrange("e d h -> d e h")
    w2_dram = W2.rearrange("e (c p) d -> p e c d", p=P)
    bg_row = bg.rearrange("(o e) -> o e", o=1)
    buf = nc.dram_tensor("sorted_rows", (SLOTS * P, ROW), F32, kind="Internal").ap()

    ctx = ExitStack()
    with ctx:
        def sb(name, shape, dt=F32):
            return ctx.enter_context(nc.sbuf_tensor(name, shape, dt))

        def sem(name):
            return ctx.enter_context(nc.semaphore(name))

        x_all = sb("x_all", [P, NT * D])
        xn_all = sb("xn_all", [P, NT * D])
        xnT_all = sb("xnT_all", [P, NT * P])
        v_all = sb("v_all", [P, NT * VW])
        w1_all = sb("w1_all", [P, E * H])
        w1_hi = [sb(f"w1_hi{c}", [P, E * P], F16) for c in range(HC)]
        w1_lo = [sb(f"w1_lo{c}", [P, E * P], F16) for c in range(HC)]
        w2_sb = [sb(f"w2_sb{c}", [P, E * D]) for c in range(HC)]
        wvg = sb("wvg", [P, VW])
        wq_sb = sb("wq_sb", [P, DQ])
        wk_sb = sb("wk_sb", [P, DQ])
        wqT = sb("wqT", [DQ, P])
        wkT = sb("wkT", [DQ, P])
        a_sb = sb("a_sb", [P, P])
        bg_sb = sb("bg_sb", [P, E])
        ident = sb("ident", [P, P])
        mask = sb("mask", [P, 2 * P])
        stats = sb("stats", [P, 2, GROUP, 6])
        moments = sb("moments", [P, 4, GROUP, 2])
        var_eps = sb("var_eps", [P, 4, GROUP])
        rstd = sb("rstd", [P, 4, GROUP])
        neg_half = sb("neg_half", [P, GROUP])
        xn_ring = sb("xn_ring", [P, 2, GROUP * D])
        xnT_ring = sb("xnT_ring", [P, 2, GROUP * P])
        logits = xn_ring[:, 0, 0:NT * E]
        taken = [0]

        def in_x_all(*shape):
            size = 1
            for n in shape:
                size *= n
            view = x_all[:, taken[0]:taken[0] + size]
            taken[0] += size
            if len(shape) == 2:
                return view.rearrange("p (a b) -> p a b", a=shape[0])
            return view

        first_key = sb("first_key", [P, E])
        best = sb("best", [P, NT])
        is_best = in_x_all(NT, E)
        chosen = in_x_all(E, NT)
        running = in_x_all(E, NT)
        zeros = sb("zeros", [P, E * NT])
        row_tot = sb("row_tot", [P, E])
        before = sb("before", [P, E])
        below = sb("below", [P, P])
        ones = sb("ones", [P, P])
        total = sb("total", [P, E])
        total_i = sb("total_i", [P, E], I32)
        tiles_i = sb("tiles_i", [P, E], I32)
        tiles = sb("tiles", [P, E])
        tiles_end = sb("tiles_end", [P, E])
        base = sb("base", [P, E])
        cum_total = sb("cum_total", [P, E])
        pads_before = sb("pads_before", [P, E])
        offset = sb("offset", [P, E])
        pos_f = sb("pos_f", [P, NT])
        ids = sb("ids", [P, NT, 2], I32)
        pairs_i = sb("pairs_i", [P, E], I32)
        pairs = sb("pairs", [P, E])
        pairs_end = sb("pairs_end", [P, E])
        odd = sb("odd", [P, E])
        pair_no = sb("pair_no", [P, PAIRS + 2])
        pair_ge = in_x_all(PAIRS + 2, E)
        expert = sb("expert", [P, PAIRS + 2])
        skipped = sb("skipped", [P, PAIRS])
        experts_i = sb("experts_i", [P, PAIRS + 1], I32)
        pair_tile = sb("pair_tile", [P, 2, PAIRS])
        tile_ge = in_x_all(2 * PAIRS, E)
        tile_expert = sb("tile_expert", [P, 2, PAIRS])
        pair_row_i = sb("pair_row_i", [P, PAIRS], I32)
        void_i = sb("void_i", [P, PAIRS, 2], I32)
        pad_no = sb("pad_no", [P, NPAD])
        pad_ge = sb("pad_ge", [P, NPAD, E])
        pad_f = sb("pad_f", [P, NPAD])
        pad_i = sb("pad_i", [P, NPAD], I32)
        pad_row = sb("pad_row", [P, ROW])
        w_sum = sb("w_sum", [P, HC])
        w_top = sb("w_top", [P, 1])
        w_pow = sb("w_pow", [P, 1])
        w_recip = sb("w_recip", [P, 1])
        w_scale = sb("w_scale", [P, 1])
        h_scale = sb("h_scale", [P, 1])
        RB = 4
        y_sb = sb("y_sb", [P, 2, T])
        masked = in_x_all(2, 3 * P)
        neg_max = sb("neg_max", [P, 2, TB])
        probs = xnT_ring[:, :, 0:3 * P]
        prob_sum = sb("prob_sum", [P, 4, TB])
        inv_sum = sb("inv_sum", [P, 2, TB])
        probsT = sb("probsT", [P, 2, 3 * P])
        rows = in_x_all(RB * TB, ROW + 1)
        RC = 6
        tile_in = x_all[:, 0:RC * 2 * ROW].rearrange("p (s h r) -> p s h r", s=RC, h=2)
        xs_hi = sb("xs_hi", [P, 2, 2 * P], F16)
        xs_lo = sb("xs_lo", [P, 2, 2 * P], F16)
        out_ids = sb("out_ids", [P, RC, 2], I32)
        hidden = xnT_all[:, 0:4 * H].rearrange("p (s c t) -> p s c t", s=2, c=HC)
        tanh_y, y_gate, y_att = (
            xnT_all[:, 4 * H + i * 4 * D:4 * H + (i + 1) * 4 * D].rearrange("p (s t) -> p s t", s=2)
            for i in range(3))
        tile_out = xnT_all[:, 4 * H + 12 * D:4 * H + (12 + 2 * RC) * D].rearrange(
            "p (s h d) -> p s h d", s=RC, h=2)

        bank = [ctx.enter_context(nc.psum_tensor(f"bank{i}", [P, 512], F32)) for i in range(8)]

        w_loaded = sem("w_loaded")
        w1_loaded = sem("w1_loaded")
        w2_loaded = sem("w2_loaded")
        x_loaded = [sem(f"x_loaded{i}") for i in range(4)]
        const_step = sem("const_step")
        consts_ready = sem("consts_ready")
        wT_done = sem("wT_done")
        wT_copied = sem("wT_copied")
        a_done = sem("a_done")
        a_ready = sem("a_ready")
        stats_done = sem("stats_done")
        moments_ready = sem("moments_ready")
        eps_added = sem("eps_added")
        rstd_ready = sem("rstd_ready")
        xn_ready = sem("xn_ready")
        xn_stored = [sem(f"xn_stored{i}") for i in range(2)]
        xnT_done = sem("xnT_done")
        xnT_ready = sem("xnT_ready")
        xnT_stored = sem("xnT_stored")
        v_done = sem("v_done")
        v_ready = sem("v_ready")
        route_step = sem("route_step")
        counts_in = sem("counts_in")
        counts_done = sem("counts_done")
        places_ready = sem("places_ready")
        experts_ready = sem("experts_ready")
        pair_rows_ready = sem("pair_rows_ready")
        voids_ready = sem("voids_ready")
        pads_ready = sem("pads_ready")
        w_summed = sem("w_summed")
        scale_ready = sem("scale_ready")
        w_split = sem("w_split")
        hi_ready = sem("hi_ready")
        y_done = sem("y_done")
        y_ready = sem("y_ready")
        scores_done = sem("scores_done")
        masked_ready = sem("masked_ready")
        probs_ready = sem("probs_ready")
        probsT_done = sem("probsT_done")
        probsT_ready = sem("probsT_ready")
        att_done = sem("att_done")
        inv_ready = sem("inv_ready")
        row_x = [sem(f"row_x{i}") for i in range(RB)]
        row_xn = sem("row_xn")
        row_ids = sem("row_ids")
        row_att = sem("row_att")
        row_sent = [sem(f"row_sent{i}") for i in range(RB)]
        pads_sent = sem("pads_sent")
        in_loaded = [sem(f"in_loaded{i}") for i in range(RC)]
        xsT_done = sem("xsT_done")
        xs_hi_ready = sem("xs_hi_ready")
        xs_lo_ready = sem("xs_lo_ready")
        up_done = sem("up_done")
        hidden_ready = sem("hidden_ready")
        down_done = sem("down_done")
        tanh_ready = sem("tanh_ready")
        gate_ready = sem("gate_ready")
        gated_ready = sem("gated_ready")
        out_ready = sem("out_ready")
        ids_ready = sem("ids_ready")
        out_sent = [sem(f"out_sent{i}") for i in range(RC)]

        def steady(eng, *waits):
            counts = [n if isinstance(n, int) else eng.to_reg(n) for _, n in waits]
            eng.wait_ge(consts_ready, 3)
            for (s, _), n in zip(waits, counts):
                eng.wait_ge(s, n)

        block = ctx.enter_context(nc.Block())

        @block.sync
        def _(sp):
            def load_x(g, turn, slot, least):
                if least >= 4:
                    sp.wait_ge(x_loaded[slot], 16 * turn)
                sp.dma_start(x_all[:, bass.ds(g * (GROUP * D), GROUP * D)],
                             x_tiles[:, bass.ds(g * GROUP, GROUP), :]).then_inc(x_loaded[slot], 16)

            def load_row_x(i, turn, slot, least):
                if least >= RB:
                    sp.wait_ge(row_sent[slot], 16 * TB * turn)
                sp.dma_start(rows[:, slot * TB:(slot + 1) * TB, 0:D],
                             x_tiles[:, bass.ds(i * TB, TB), :]).then_inc(row_x[slot], 16)

            def load_pair(k, turn, slot, least):
                if least >= RC:
                    sp.wait_ge(out_sent[slot], 32 * turn)
                row = nc.values_load(pair_row_i[0:1, bass.ds(k, 1)], engines=[sp.engine], min_val=0,
                                     max_val=(SLOTS - 2) * P,
                                     skip_runtime_bounds_check_because="at most the last pair's row")
                sp.dma_start(tile_in[:, slot, :, :],
                             buf[bass.ds(row, 2 * P), :].rearrange("(h p) r -> p h r", p=P)
                             ).then_inc(in_loaded[slot], 16)

            def load_rest(g, turn, slot, least):
                if least >= 2:
                    load_x(g, turn, slot, least)

            for g in range(2):
                load_x(g, 0, g, 0)
            sp.dma_start(wvg[:, 0:D], Wv).then_inc(w_loaded, 16)
            sp.dma_start(wvg[:, D:VW], Wg).then_inc(w_loaded, 16)
            sp.dma_start(wq_sb[:, :], Wq).then_inc(w_loaded, 16)
            sp.dma_start(wk_sb[:, :], Wk).then_inc(w_loaded, 16)
            sp.dma_start(bg_sb[:, :], bg_row.partition_broadcast(P)).then_inc(w_loaded, 16)
            pipeline(sp, NG, 4, 4, [(0, load_rest)])
            sp.dma_start(w1_all[:, :].rearrange("p (e h) -> p e h", e=E), w1_dram).then_inc(w1_loaded, 16)
            for c in range(HC):
                sp.dma_start(w2_sb[c][:, :].rearrange("p (e d) -> p e d", d=D),
                             w2_dram[:, :, c, :]).then_inc(w2_loaded, 16)
            sp.wait_ge(xn_ready, NG)
            pipeline(sp, B, RB, RB, [(0, load_row_x)])
            sp.wait_ge(pads_sent, 16 * NPAD)
            for slot in range(RB):
                sp.wait_ge(row_sent[slot], 16 * TB * (B // RB))
            sp.wait_ge(pair_rows_ready, 1)
            pipeline(sp, PAIRS, RC, RC, [(0, load_pair)])
            for slot in range(RC):
                sp.wait_ge(out_sent[slot], 32 * len(range(slot, PAIRS, RC)))

        @block.gpsimd
        def _(pool):
            pool.memset(neg_half[:, :], -0.5)
            pool.memset(ones[:, :], 1.0)
            pool.memset(ident[:, :], 0.0).then_inc(const_step, 1)
            pool.memset(mask[:, :], 0.0).then_inc(const_step, 1)
            pool.memset(below[:, :], 1.0).then_inc(const_step, 1)
            pool.wait_ge(const_step, 3)
            pool.affine_select(out=ident[:, :], in_=ident[:, :], compare_op=ALU.not_equal, fill=1.0,
                               base=0, pattern=[[-1, P]], channel_multiplier=1).then_inc(consts_ready, 1)
            pool.affine_select(out=mask[:, P:2 * P], in_=mask[:, P:2 * P], compare_op=ALU.is_ge, fill=-BIG,
                               base=0, pattern=[[-1, P]], channel_multiplier=1).then_inc(consts_ready, 1)
            pool.affine_select(out=below[:, :], in_=below[:, :], compare_op=ALU.is_gt, fill=0.0,
                               base=0, pattern=[[1, P]], channel_multiplier=-1).then_inc(consts_ready, 1)

            pool.iota(ids[:, :, 0], pattern=[[P, NT]], base=0, channel_multiplier=1).then_inc(consts_ready, 1)
            pool.memset(zeros[:, :], 0.0)
            pool.memset(pad_row[:, 0:3 * D], 0.0)
            pool.memset(pad_row[:, 3 * D:ROW].bitcast(I32), TOKENS)
            for e in range(E):
                pool.memset(first_key[:, e:e + 1], float(E - e))
            pool.iota(pad_no[:, :], pattern=[[P, NPAD]], base=0, channel_multiplier=1,
                      allow_small_or_imprecise_dtypes=True)
            pool.iota(pair_no[:, :], pattern=[[1, PAIRS + 2]], base=-1, channel_multiplier=0,
                      allow_small_or_imprecise_dtypes=True).then_inc(consts_ready, 1)

            def rstd_of(g, turn, slot, least):
                steady(pool, (moments_ready, g + 1))
                pool.tensor_scalar(var_eps[:, slot, :], moments[:, slot, :, 1], EPS, None,
                                   ALU.add).then_inc(eps_added, 1)
                pool.wait_ge(eps_added, g + 1)
                pool.tensor_tensor(rstd[:, slot, :], var_eps[:, slot, :], neg_half[:, :],
                                   ALU.pow).then_inc(rstd_ready, 1)

            pool.wait_ge(consts_ready, 3)
            pipeline(pool, NG, 4, 4, [(0, rstd_of)])
            pool.wait_ge(pads_ready, 1)
            for m in range(NPAD):
                pool.indirect_dma_start(out=buf[:, :], in_=pad_row[:, :], in_offset=None,
                                        out_offset=bass.IndirectOffsetOnAxis(ap=pad_i[:, m:m + 1], axis=0),
                                        bounds_check=SLOTS * P - 1,
                                        oob_is_err=False).then_inc(pads_sent, 16)

            def send(i, turn, slot, least):
                steady(pool, (row_x[slot], 16 * (turn + 1)), (row_xn, i + 1), (row_ids, i + 1),
                       (row_att, i + 1))
                for h in range(TB):
                    r = rows[:, slot * TB + h, :]
                    pool.indirect_dma_start(
                        out=buf[:, :], in_=r[:, 0:ROW], in_offset=None,
                        out_offset=bass.IndirectOffsetOnAxis(ap=r[:, ROW:ROW + 1].bitcast(I32), axis=0),
                        bounds_check=SLOTS * P - 1, oob_is_err=False).then_inc(row_sent[slot], 16)

            pipeline(pool, B, RB, RB, [(0, send)])

            def send_out(k, turn, slot, least):
                steady(pool, (out_ready, k + 1), (ids_ready, k + 1))
                for h in range(2):
                    pool.indirect_dma_start(
                        out=out_rows, in_=tile_out[:, slot, h, :], in_offset=None,
                        out_offset=bass.IndirectOffsetOnAxis(ap=out_ids[:, slot, h:h + 1], axis=0),
                        bounds_check=TOKENS - 1, oob_is_err=False).then_inc(out_sent[slot], 16)

            pipeline(pool, PAIRS, RC, RC, [(0, send_out)])

        @block.scalar
        def _(act):
            act.wait_ge(wT_done, 2)
            act.copy(wqT[:, :], bank[7][0:DQ, 0:P]).then_inc(wT_copied, 1)
            act.copy(wkT[:, :], bank[7][0:DQ, P:2 * P]).then_inc(wT_copied, 1)
            act.wait_ge(a_done, 1)
            act.copy(a_sb[:, :], bank[7][:, 2 * P:3 * P]).then_inc(a_ready, 1)

            def xnT_out(g, turn, slot, least):
                act.wait_ge(xnT_done, g + 1)
                if least >= 2:
                    act.wait_ge(v_done, g - 1)
                act.copy(xnT_ring[:, slot % 2, :], bank[slot % 2][:, :]).then_inc(xnT_ready, 1)
                act.copy(xnT_all[:, bass.ds(g * (GROUP * P), GROUP * P)],
                         bank[slot % 2][:, :]).then_inc(xnT_stored, 1)
                act.wait_ge(xn_ready, g + 1)
                act.dma_start(xn_all[:, bass.ds(g * (GROUP * D), GROUP * D)],
                              xn_ring[:, slot % 2, :]).then_inc(xn_stored[slot % 2], 16)

            def v_out(g, turn, slot, least):
                act.wait_ge(v_done, g + 1)
                for h in range(2):
                    last = act.copy(v_all[:, bass.ds(g * (GROUP * VW) + h * 2 * VW, 2 * VW)],
                                    bank[2 + 2 * (slot % 2) + h][:, 0:2 * VW])
                last.then_inc(v_ready, 1)

            pipeline(act, NG, 4, 4, [(0, xnT_out), (1, v_out)])
            act.wait_ge(w1_loaded, 16)
            for q in range(HC):
                last = act.activation(w1_lo[q][:, :], w1_all[:, q * E * P:(q + 1) * E * P], ACT.Abs,
                                      accum_out=w_sum[:, q:q + 1])
            last.then_inc(w_summed, 1)
            act.wait_ge(scale_ready, 1)

            def y_out(i, turn, slot, least):
                act.wait_ge(y_done, i + 1)
                if least >= 2:
                    act.wait_ge(scores_done, i - 1)
                act.copy(y_sb[:, slot % 2, :],
                         bank[6 + slot % 2][:, 0:T]).then_inc(y_ready, 1)

            def softmax(i, turn, slot, least):
                s = slot % 2
                act.wait_ge(masked_ready, i + 1)
                if least >= 2:
                    act.wait_ge(probsT_done, i - 1)
                if least >= 4:
                    act.wait_ge(inv_ready, i - 3)
                act.activation(probs[:, s, 0:P], masked[:, s, 0:P], ACT.Exp, bias=neg_max[:, s, 0:1],
                               scale=-1.0, accum_out=prob_sum[:, slot, 0:1])
                act.activation(probs[:, s, P:3 * P], masked[:, s, P:3 * P], ACT.Exp, bias=neg_max[:, s, 1:2],
                               scale=-1.0, accum_out=prob_sum[:, slot, 1:2]).then_inc(probs_ready, 1)

            def rest(i, turn, slot, least):
                if least >= RB:
                    act.wait_ge(row_sent[slot], 16 * TB * turn)
                act.copy(rows[:, slot * TB:(slot + 1) * TB, D:2 * D],
                         xn_all[:, bass.ds(i * (TB * D), TB * D)].rearrange("p (n d) -> p n d", d=D)
                         ).then_inc(row_xn, 1)
                act.activation(w1_hi[slot][:, bass.ds(turn * P, P)], w1_all[:, bass.ds(i * P, P)], ACT.Copy,
                               scale=w_scale[:, 0:1]).then_inc(hi_ready, 1)

            pipeline(act, B, 4, 8, [(0, y_out), (1, softmax), (2, rest)])

            def gelu(k, turn, slot, least):
                s = slot % 2
                if least >= 2:
                    act.wait_ge(down_done, k - 1)
                for q in range(2):
                    act.wait_ge(up_done, 2 * k + q + 1)
                    act.activation(hidden[:, s, 2 * q:2 * q + 2, :].rearrange("p c t -> p (c t)"),
                                   bank[2 * s + q][:, :], ACT.Gelu_apprx_tanh,
                                   scale=h_scale[:, 0:1]).then_inc(hidden_ready, 1)

            def tanh(k, turn, slot, least):
                s = slot % 2
                act.wait_ge(down_done, k + 1)
                if least >= 2:
                    act.wait_ge(gate_ready, k - 1)
                act.activation(tanh_y[:, s, :], bank[4 + s][:, 0:2 * D], ACT.Tanh,
                               scale=0.5).then_inc(tanh_ready, 1)

            pipeline(act, PAIRS, 4, 4, [(0, gelu), (1, tanh)])

        @block.vector
        def _(dve):
            def stats_of(g, turn, slot, least):
                dve.wait_ge(x_loaded[slot], 16 * (turn + 1))
                if least >= 2:
                    dve.wait_ge(moments_ready, g - 1)
                for j in range(GROUP):
                    last = dve.bn_stats(stats[:, slot % 2, j, :],
                                        x_all[:, bass.ds(g * (GROUP * D) + j * D, D)])
                last.then_inc(stats_done, 1)
                if least >= 4:
                    dve.wait_ge(xn_ready, g - 3)
                    dve.wait_ge(eps_added, g - 3)
                steady(dve, (stats_done, g + 1))
                for j in range(GROUP):
                    last = dve.bn_aggr(moments[:, slot, j, :], stats[:, slot % 2, j, :])
                last.then_inc(moments_ready, 1)

            def normalise(g, turn, slot, least):
                dve.wait_ge(rstd_ready, g + 1)
                dve.wait_ge(moments_ready, g + 1)
                if least >= 2:
                    dve.wait_ge(xnT_done, g - 1)
                    dve.wait_ge(xn_stored[slot % 2], 8 * (g - slot % 2))
                for j in range(GROUP):
                    last = dve.tensor_scalar(xn_ring[:, slot % 2, j * D:(j + 1) * D],
                                             x_all[:, bass.ds(g * (GROUP * D) + j * D, D)],
                                             moments[:, slot, j, 0:1], rstd[:, slot, j:j + 1],
                                             ALU.subtract, ALU.mult)
                last.then_inc(xn_ready, 1)

            dve.wait_ge(consts_ready, 3)
            pipeline(dve, NG, 4, 4, [(0, stats_of), (1, normalise)])

            steps = [0]

            def then(ins):
                steps[0] += 1
                ins.then_inc(route_step, 1)
                dve.wait_ge(route_step, steps[0])

            lg = logits.rearrange("p (n e) -> p n e", e=E)
            chosen_flat = chosen[:, :, :].rearrange("p e n -> p (e n)")
            running_flat = running[:, :, :].rearrange("p e n -> p (e n)")
            by_tile = chosen[:, :, :].rearrange("p e n -> p n e")
            run_by_tile = running[:, :, :].rearrange("p e n -> p n e")
            dve.wait_ge(v_ready, NG)
            dve.wait_ge(xn_stored[0], 16 * NG // 2)
            dve.wait_ge(xn_stored[1], 16 * NG // 2)
            dve.wait_ge(consts_ready, 5)
            dve.wait_ge(w_loaded, 80)
            then(dve.tensor_tensor(lg, v_all[:, :].rearrange("p (n v) -> p n v", v=VW)[:, :, D:VW],
                                   bg_sb[:, None, :].broadcast_to([P, NT, E]), ALU.add))
            then(dve.tensor_reduce(best[:, :], lg, AX.X, ALU.max))
            then(dve.tensor_tensor(is_best[:, :, :], lg, best[:, :, None].broadcast_to([P, NT, E]), ALU.is_ge))
            then(dve.tensor_tensor(is_best[:, :, :], is_best[:, :, :],
                                   first_key[:, None, :].broadcast_to([P, NT, E]), ALU.mult))
            then(dve.tensor_reduce(best[:, :], is_best[:, :, :], AX.X, ALU.max))
            then(dve.tensor_tensor(by_tile, first_key[:, None, :].broadcast_to([P, NT, E]),
                                   best[:, :, None].broadcast_to([P, NT, E]), ALU.is_equal))
            then(dve.tensor_tensor_scan(running_flat, zeros[:, :], chosen_flat, 0.0, ALU.add, ALU.add))
            dve.memset(before[:, 0:1], 0.0)
            then(dve.tensor_copy(before[:, 1:E], running[:, 0:E - 1, NT - 1]))
            then(dve.tensor_tensor(row_tot[:, :], running[:, :, NT - 1], before[:, :], ALU.subtract))
            dve.engine_nop().then_inc(counts_in, 1)
            dve.wait_ge(counts_done, 1)
            lower = bank[5][:, 0:E]
            then(dve.tensor_copy(total[:, :], bank[5][:, E:2 * E]))
            then(dve.tensor_scalar(total_i[:, :], total[:, :], float(P - 1), None, ALU.add))
            then(dve.tensor_scalar(tiles_i[:, :], total_i[:, :], 7, None, ALU.arith_shift_right))
            then(dve.tensor_copy(tiles[:, :], tiles_i[:, :]))
            then(dve.tensor_tensor_scan(tiles_end[:, :], zeros[:, 0:E], tiles[:, :], 0.0, ALU.add, ALU.add))
            then(dve.tensor_tensor(base[:, :], tiles_end[:, :], tiles[:, :], ALU.subtract))
            then(dve.tensor_scalar(base[:, :], base[:, :], float(P), None, ALU.mult))
            then(dve.tensor_tensor(offset[:, :], base[:, :], before[:, :], ALU.subtract))
            then(dve.scalar_tensor_tensor(offset[:, :], offset[:, :], -1.0, lower, ALU.add, ALU.add))
            then(dve.tensor_tensor(run_by_tile, run_by_tile, offset[:, None, :].broadcast_to([P, NT, E]), ALU.add))
            then(dve.tensor_tensor(running_flat, running_flat, chosen_flat, ALU.mult))
            then(dve.tensor_reduce(pos_f[:, :], run_by_tile, AX.X, ALU.add))
            dve.tensor_copy(ids[:, :, 1], pos_f[:, :]).then_inc(places_ready, 1)
            then(dve.tensor_tensor_scan(cum_total[:, :], zeros[:, 0:E], total[:, :], 0.0, ALU.add, ALU.add))
            then(dve.tensor_tensor(cum_total[:, :], cum_total[:, :], total[:, :], ALU.subtract))
            then(dve.tensor_tensor(pads_before[:, :], base[:, :], cum_total[:, :], ALU.subtract))
            then(dve.tensor_tensor(pad_ge[:, :, :], pad_no[:, :, None].broadcast_to([P, NPAD, E]),
                                   pads_before[:, None, :].broadcast_to([P, NPAD, E]), ALU.is_ge))
            then(dve.tensor_tensor(pad_ge[:, :, :], pad_ge[:, :, :],
                                   total[:, None, :].broadcast_to([P, NPAD, E]), ALU.mult))
            then(dve.tensor_reduce(pad_f[:, :], pad_ge[:, :, :], AX.X, ALU.add))
            dve.tensor_tensor(pad_i[:, :], pad_f[:, :], pad_no[:, :], ALU.add).then_inc(pads_ready, 1)
            then(dve.tensor_scalar(pairs_i[:, :], tiles_i[:, :], 1, None, ALU.add))
            then(dve.tensor_scalar(pairs_i[:, :], pairs_i[:, :], 1, None, ALU.arith_shift_right))
            then(dve.tensor_copy(pairs[:, :], pairs_i[:, :]))
            then(dve.tensor_tensor_scan(pairs_end[:, :], zeros[:, 0:E], pairs[:, :], 0.0, ALU.add, ALU.add))
            then(dve.scalar_tensor_tensor(odd[:, :], pairs[:, :], 2.0, tiles[:, :], ALU.mult, ALU.subtract))
            then(dve.tensor_tensor(pair_ge[:, :, :], pair_no[:, :, None].broadcast_to([P, PAIRS + 2, E]),
                                   pairs_end[:, None, :].broadcast_to([P, PAIRS + 2, E]), ALU.is_ge))
            then(dve.tensor_reduce(expert[:, :], pair_ge[:, :, :], AX.X, ALU.add))
            then(dve.tensor_scalar(expert[:, :], expert[:, :], float(E - 1), None, ALU.min))
            dve.scalar_tensor_tensor(experts_i[:, :], expert[:, 1:PAIRS + 2], float(E),
                                     expert[:, 0:PAIRS + 1], ALU.mult, ALU.add).then_inc(experts_ready, 1)
            then(dve.tensor_tensor(pair_ge[:, :, :], pair_ge[:, :, :],
                                   odd[:, None, :].broadcast_to([P, PAIRS + 2, E]), ALU.mult))
            then(dve.tensor_reduce(skipped[:, :], pair_ge[:, 1:PAIRS + 1, :], AX.X, ALU.add))
            then(dve.scalar_tensor_tensor(pair_tile[:, 0, :], pair_no[:, 1:PAIRS + 1], 2.0, skipped[:, :],
                                          ALU.mult, ALU.subtract))
            then(dve.tensor_scalar(pair_tile[:, 1, :], pair_tile[:, 0, :], 1.0, None, ALU.add))
            then(dve.tensor_scalar(skipped[:, :], pair_tile[:, 0, :], float(SLOTS - 2), float(P), ALU.min,
                                   ALU.mult))
            dve.tensor_copy(pair_row_i[:, :], skipped[:, :]).then_inc(pair_rows_ready, 1)
            then(dve.tensor_tensor(
                tile_ge[:, :, :],
                pair_tile[:, :, :].rearrange("p h m -> p (h m)")[:, :, None].broadcast_to([P, 2 * PAIRS, E]),
                tiles_end[:, None, :].broadcast_to([P, 2 * PAIRS, E]), ALU.is_ge))
            then(dve.tensor_reduce(tile_expert[:, :, :].rearrange("p h m -> p (h m)"), tile_ge[:, :, :], AX.X,
                                   ALU.add))
            then(dve.tensor_tensor(tile_expert[:, :, :], tile_expert[:, :, :],
                                   expert[:, None, 1:PAIRS + 1].broadcast_to([P, 2, PAIRS]), ALU.is_gt))
            dve.tensor_scalar(void_i[:, :, :].rearrange("p m h -> p h m"), tile_expert[:, :, :],
                              float(VOID), None, ALU.mult).then_inc(voids_ready, 1)
            dve.wait_ge(counts_done, 2)
            then(dve.tensor_reduce(w_top[:, :], bank[4][:, 0:P], AX.X, ALU.max))
            then(dve.tensor_scalar(w_top[:, :], w_top[:, :], 1e-30, None, ALU.max))
            then(dve.tensor_scalar(w_pow[:, :].bitcast(I32), w_top[:, :].bitcast(I32), 0x7F800000, None,
                                   ALU.bitwise_and))
            then(dve.reciprocal(w_recip[:, :], w_pow[:, :]))
            then(dve.tensor_scalar(h_scale[:, :], w_pow[:, :], 1.0 / (W_TOP * XN_SCALE), None, ALU.mult))
            dve.tensor_scalar(w_scale[:, :], w_recip[:, :], W_TOP, None, ALU.mult).then_inc(scale_ready, 1)
            dve.wait_ge(scale_ready, 1)
            dve.wait_ge(places_ready, 1)

            def mask_max(i, turn, slot, least):
                s = slot % 2
                if least >= 2:
                    dve.wait_ge(probs_ready, i - 1)
                steady(dve, (scores_done, i + 1))
                dve.tensor_tensor_reduce(masked[:, s, 0:P], bank[s][:, 0:P], mask[:, P:2 * P],
                                         -(DQ ** -0.5), BIG, ALU.add, ALU.min, neg_max[:, s, 0:1])
                dve.tensor_tensor_reduce(masked[:, s, P:3 * P], bank[s][:, P:3 * P], mask[:, :],
                                         -(DQ ** -0.5), BIG, ALU.add, ALU.min,
                                         neg_max[:, s, 1:2]).then_inc(masked_ready, 1)

            def probsT_out(i, turn, slot, least):
                s = slot % 2
                dve.wait_ge(probsT_done, i + 1)
                if least >= 2:
                    dve.wait_ge(att_done, i - 1)
                dve.tensor_copy(probsT[:, s, :], bank[2 + s][:, 0:3 * P]).then_inc(probsT_ready, 1)

            def att_out(i, turn, slot, least):
                s = slot % 2
                dve.wait_ge(probs_ready, i + 1)
                if least >= 2:
                    dve.wait_ge(row_att, i - 1)
                dve.reciprocal(inv_sum[:, s, :], prob_sum[:, slot, :]).then_inc(inv_ready, 1)
                dve.wait_ge(hi_ready, i + 1)
                dve.scalar_tensor_tensor(w1_lo[slot][:, bass.ds(turn * P, P)], w1_all[:, bass.ds(i * P, P)],
                                         w_scale[:, 0:1], w1_hi[slot][:, bass.ds(turn * P, P)], ALU.mult,
                                         ALU.subtract).then_inc(w_split, 1)
                if least >= RB:
                    dve.wait_ge(row_sent[slot], 16 * TB * turn)
                r = rows[:, slot * TB:(slot + 1) * TB, :]
                dve.tensor_copy(r[:, :, 3 * D:3 * D + 2].bitcast(I32),
                                ids[:, bass.ds(i * TB, TB), :]).then_inc(row_ids, 1)
                dve.wait_ge(att_done, i + 1)
                dve.wait_ge(inv_ready, i + 1)
                dve.tensor_tensor(r[:, :, 2 * D:3 * D],
                                  bank[4 + s][:, 0:T].rearrange("p (n d) -> p n d", d=D),
                                  inv_sum[:, s, :, None].broadcast_to([P, TB, D]),
                                  ALU.mult).then_inc(row_att, 1)

            pipeline(dve, B, 4, 8, [(0, mask_max), (1, probsT_out), (2, att_out)])

            def split_xs(k, turn, slot, least):
                s = slot % 2
                dve.wait_ge(xsT_done, k + 1)
                if least >= 2:
                    dve.wait_ge(up_done, 2 * (k - 1))
                xsT = bank[6 + s][:, 0:2 * P]
                dve.tensor_scalar(xs_hi[:, s, :], xsT, XN_SCALE, None, ALU.mult).then_inc(xs_hi_ready, 1)
                if least >= RC:
                    dve.wait_ge(out_sent[slot], 32 * turn)
                dve.wait_ge(in_loaded[slot], 16 * (turn + 1))
                dve.tensor_tensor(out_ids[:, slot, :], tile_in[:, slot, :, 3 * D].bitcast(I32),
                                  void_i[:, bass.ds(k, 1), :].rearrange("p m h -> p (m h)"),
                                  ALU.bitwise_or).then_inc(ids_ready, 1)
                dve.wait_ge(xs_hi_ready, k + 1)
                dve.scalar_tensor_tensor(xs_lo[:, s, :], xsT, XN_SCALE, xs_hi[:, s, :], ALU.mult,
                                         ALU.subtract).then_inc(xs_lo_ready, 1)

            def combine(k, turn, slot, least):
                s = slot % 2
                dve.wait_ge(tanh_ready, k + 1)
                if least >= 2:
                    dve.wait_ge(gated_ready, k - 1)
                dve.scalar_tensor_tensor(y_gate[:, s, :], tanh_y[:, s, :], 1.0,
                                         bank[4 + s][:, 0:2 * D], ALU.add,
                                         ALU.mult).then_inc(gate_ready, 1)
                dve.wait_ge(gate_ready, k + 1)
                if least >= 2:
                    dve.wait_ge(out_ready, k - 1)
                halves = "p (h d) -> p h d"
                dve.tensor_tensor(y_att[:, s, :].rearrange(halves, h=2),
                                  y_gate[:, s, :].rearrange(halves, h=2), tile_in[:, slot, :, 2 * D:3 * D],
                                  ALU.mult).then_inc(gated_ready, 1)
                dve.wait_ge(gated_ready, k + 1)
                if least >= RC:
                    dve.wait_ge(out_sent[slot], 32 * turn)
                dve.scalar_tensor_tensor(tile_out[:, slot, :, :], y_att[:, s, :].rearrange(halves, h=2), 0.5,
                                         tile_in[:, slot, :, 0:D], ALU.mult,
                                         ALU.add).then_inc(out_ready, 1)

            dve.wait_ge(voids_ready, 1)
            pipeline(dve, PAIRS, RC, RC + 3, [(0, split_xs), (3, combine)])

        @block.tensor
        def _(pe):
            pe.wait_ge(consts_ready, 3)
            pe.wait_ge(w_loaded, 80)
            pe.transpose(bank[7][0:DQ, 0:P], wq_sb[:, :], ident[:, :]).then_inc(wT_done, 1)
            pe.transpose(bank[7][0:DQ, P:2 * P], wk_sb[:, :], ident[:, :]).then_inc(wT_done, 1)
            pe.wait_ge(wT_copied, 2)
            pe.matmul(bank[7][:, 2 * P:3 * P], wqT[:, :], wkT[:, :], start=True, stop=True).then_inc(a_done, 1)

            def xnT_of(g, turn, slot, least):
                pe.wait_ge(xn_ready, g + 1)
                if least >= 2:
                    pe.wait_ge(xnT_stored, g - 1)
                for j in range(GROUP):
                    last = pe.transpose(bank[slot % 2][:, j * P:(j + 1) * P],
                                        xn_ring[:, slot % 2, j * D:(j + 1) * D], ident[:, :])
                last.then_inc(xnT_done, 1)

            def v_of(g, turn, slot, least):
                pe.wait_ge(xnT_ready, g + 1)
                if least >= 2:
                    pe.wait_ge(v_ready, g - 1)
                for j in range(GROUP):
                    b = bank[2 + 2 * (slot % 2) + j // 2]
                    last = pe.matmul(b[:, (j % 2) * VW:(j % 2 + 1) * VW],
                                     xnT_ring[:, slot % 2, j * P:(j + 1) * P], wvg[:, :],
                                     start=True, stop=True)
                last.then_inc(v_done, 1)

            pipeline(pe, NG, 4, 4, [(0, xnT_of), (1, v_of)])

            pe.wait_ge(a_ready, 1)
            pe.wait_ge(counts_in, 1)
            pe.matmul(bank[5][:, 0:E], below[:, :], row_tot[:, :], start=True, stop=True)
            pe.matmul(bank[5][:, E:2 * E], ones[:, :], row_tot[:, :], start=True,
                      stop=True).then_inc(counts_done, 1)
            pe.wait_ge(w_summed, 1)
            for q in range(HC):
                last = pe.matmul(bank[4][:, 0:P], w_sum[:, q:q + 1].broadcast_to([P, P]), ident[:, :],
                                 start=(q == 0), stop=(q == HC - 1))
            last.then_inc(counts_done, 1)
            pe.wait_ge(v_ready, NG)
            pe.wait_ge(xnT_stored, NG)

            def y_of(i, turn, slot, least):
                if least >= 2:
                    pe.wait_ge(y_ready, i - 1)
                pe.matmul(bank[6 + slot % 2][:, 0:T], a_sb[:, :],
                          xnT_all[:, bass.ds(i * T, T)], start=True, stop=True).then_inc(y_done, 1)

            def scores_of(i, turn, slot, least):
                s = slot % 2
                pe.wait_ge(y_ready, i + 1)
                if least >= 2:
                    pe.wait_ge(masked_ready, i - 1)
                pe.matmul(bank[s][:, 0:P], y_sb[:, s, 0:P], xnT_all[:, bass.ds(i * T, P)],
                          start=True, stop=True)
                pe.matmul(bank[s][:, P:3 * P], y_sb[:, s, P:2 * P], xnT_all[:, bass.ds(i * T, T)],
                          start=True, stop=True).then_inc(scores_done, 1)

            def probsT_of(i, turn, slot, least):
                s = slot % 2
                pe.wait_ge(probs_ready, i + 1)
                if least >= 2:
                    pe.wait_ge(probsT_ready, i - 1)
                for j in range(3):
                    last = pe.transpose(bank[2 + s][:, j * P:(j + 1) * P], probs[:, s, j * P:(j + 1) * P],
                                        ident[:, :])
                last.then_inc(probsT_done, 1)

            def att_of(i, turn, slot, least):
                s = slot % 2
                pe.wait_ge(probsT_ready, i + 1)
                if least >= 2:
                    pe.wait_ge(row_att, i - 1)
                o = bank[4 + s][:, 0:T]
                v0, v1 = (v_all[:, bass.ds(i * (TB * VW) + h * VW, D)] for h in range(TB))
                pe.matmul(o[:, 0:D], probsT[:, s, 0:P], v0, start=True, stop=True)
                pe.matmul(o[:, D:2 * D], probsT[:, s, P:2 * P], v0, start=True, stop=False)
                pe.matmul(o[:, D:2 * D], probsT[:, s, 2 * P:3 * P], v1, start=False,
                          stop=True).then_inc(att_done, 1)

            pipeline(pe, B, 4, 8, [(0, y_of), (1, scores_of), (2, probsT_of), (3, att_of)])

            pe.wait_ge(experts_ready, 1)
            pe.wait_ge(w_split, B)
            pe.wait_ge(w2_loaded, 16 * HC)

            def xsT_of(k, turn, slot, least):
                s = slot % 2
                pe.wait_ge(in_loaded[slot], 16 * (turn + 1))
                if least >= 2:
                    pe.wait_ge(xs_lo_ready, k - 1)
                for h in range(2):
                    last = pe.transpose(bank[6 + s][:, h * P:(h + 1) * P], tile_in[:, slot, h, D:2 * D],
                                        ident[:, :])
                last.then_inc(xsT_done, 1)

            def load_experts(k):
                return nc.values_load(experts_i[0:1, bass.ds(k, 1)], engines=[pe.engine], min_val=0,
                                      max_val=E * E - 1,
                                      skip_runtime_bounds_check_because="each expert is at most E - 1")

            experts = [None]

            def up(k, turn, slot, least):
                experts[0] = load_experts(k)
                own = pe.snap(experts[0] // E * P)
                s = slot % 2
                pe.wait_ge(xs_lo_ready, k + 1)
                if least >= 2:
                    pe.wait_ge(hidden_ready, 2 * (k - 1))
                for c in range(HC):
                    h = bank[2 * s + c // 2][:, c % 2 * 2 * P:(c % 2 + 1) * 2 * P]
                    hi = w1_hi[c][:, bass.ds(own, P)]
                    lo = w1_lo[c][:, bass.ds(own, P)]
                    pe.matmul(h, hi, xs_hi[:, s, :], start=True, stop=False)
                    pe.matmul(h, hi, xs_lo[:, s, :], start=False, stop=False)
                    last = pe.matmul(h, lo, xs_hi[:, s, :], start=False, stop=True)
                    if c % 2:
                        last.then_inc(up_done, 1)

            def down(k, turn, slot, least):
                if least == PAIRS - 1:
                    experts[0] = load_experts(k + 1)
                own = pe.snap(experts[0] % E * P)
                s = slot % 2
                pe.wait_ge(hidden_ready, 2 * (k + 1))
                if least >= 2:
                    pe.wait_ge(gate_ready, k - 1)
                for h in range(2):
                    for c in range(HC):
                        last = pe.matmul(bank[4 + s][:, h * D:(h + 1) * D],
                                         hidden[:, s, c, h * P:(h + 1) * P],
                                         w2_sb[c][:, bass.ds(own, D)], start=(c == 0), stop=(c == HC - 1))
                last.then_inc(down_done, 1)

            pipeline(pe, PAIRS, RC, 4, [(0, xsT_of), (1, up), (2, down)])


_INS = ['L0_attn_X', 'L0_attn_Wq', 'L0_attn_Wk', 'L0_attn_Wv', 'L0_ffn_W1', 'L0_ffn_W2', 'L0_ffn_Wg', 'L0_ffn_bg']
_OUT = ((32, 256, 128), 'float32')


def kernel(**inputs):
    import numpy as _np
    import concourse.bacc as _bacc
    from concourse import mybir as _mybir
    from concourse.bass_utils import run_bass_kernel_spmd as _run

    nc = _bacc.Bacc("TRN2", target_bir_lowering=False, num_devices=1)
    arrays, args = {}, []
    for name in _INS:
        a = _np.ascontiguousarray(inputs[name])
        arrays[f"in_{name}_dram"] = a
        args.append(nc.dram_tensor(f"in_{name}_dram", a.shape, _mybir.dt.from_np(a.dtype), kind="ExternalInput").ap())
    shape, dtype = _OUT
    args.append(nc.dram_tensor("out_dram", shape, _mybir.dt.from_np(_np.dtype(dtype)), kind="ExternalOutput").ap())
    routed_block(nc, *args)
    r = _run(nc, [arrays], core_ids=[0])
    return r.results[0]["out_dram"]
```

```python
from contextlib import ExitStack

import concourse.bass as bass
from concourse import mybir

P = 128
ALU = mybir.AluOpType
ACT = mybir.ActivationFunctionType
F32 = mybir.dt.float32
F16 = mybir.dt.float16
I32 = mybir.dt.int32
AX = mybir.AxisListType
EPS = 1e-5
BIG = 3.0e38
XN_SCALE = 1024.0
W_TOP = 16384.0


def pipeline(eng, count, unroll, warm, stages):
    last = count + max(lag for lag, _ in stages)
    lo = -(-warm // unroll) * unroll
    turns = max(0, (count - lo) // unroll)
    hi = lo + turns * unroll

    def peeled(s):
        for lag, step in stages:
            k = s - lag
            if 0 <= k < count:
                step(k, k // unroll, k % unroll, k)

    for s in range(min(lo, last) if turns else last):
        peeled(s)
    if turns:
        with eng.Fori(0, turns) as t:
            for j in range(unroll):
                for lag, step in stages:
                    k = lo + j - lag
                    step(t * unroll + k, t + k // unroll, k % unroll, k)
        for s in range(hi, last):
            peeled(s)


def routed_block(nc, X, Wq, Wk, Wv, W1, W2, Wg, bg, out):
    B, T, D = X.shape
    DQ = Wq.shape[1]
    E, _, H = W1.shape
    TOKENS = B * T
    NT = TOKENS // P
    TB = T // P
    GROUP = 4
    NG = NT // GROUP
    HC = H // P
    SLOTS = NT + E
    PAIRS = NT // 2 + E - 1
    VOID = 1 << TOKENS.bit_length()
    NPAD = SLOTS - NT
    ROW = 3 * D + 1
    VW = D + E
    assert D == P and TB == 2 and H == 4 * P

    x_tiles = X.rearrange("b (h p) d -> p (b h) d", p=P)
    out_rows = out.rearrange("b t d -> (b t) d")
    w1_dram = W1.rearrange("e d h -> d e h")
    w2_dram = W2.rearrange("e (c p) d -> p e c d", p=P)
    bg_row = bg.rearrange("(o e) -> o e", o=1)
    buf = nc.dram_tensor("sorted_rows", (SLOTS * P, ROW), F32, kind="Internal").ap()

    ctx = ExitStack()
    with ctx:
        def sb(name, shape, dt=F32):
            return ctx.enter_context(nc.sbuf_tensor(name, shape, dt))

        def sem(name):
            return ctx.enter_context(nc.semaphore(name))

        x_all = sb("x_all", [P, NT * D])
        work = sb("work", [P, NT * D])
        xnT_all = sb("xnT_all", [P, NT * P])
        v_all = sb("v_all", [P, NT * VW])
        w1_all = sb("w1_all", [P, E * H])
        w1_hi = [sb(f"w1_hi{c}", [P, E * P], F16) for c in range(HC)]
        w1_lo = [sb(f"w1_lo{c}", [P, E * P], F16) for c in range(HC)]
        w2_sb = [sb(f"w2_sb{c}", [P, E * D]) for c in range(HC)]
        wvg = sb("wvg", [P, VW])
        wq_sb = sb("wq_sb", [P, DQ])
        wk_sb = sb("wk_sb", [P, DQ])
        wqT = sb("wqT", [DQ, P])
        wkT = sb("wkT", [DQ, P])
        a_sb = sb("a_sb", [P, P])
        bg_sb = sb("bg_sb", [P, E])
        ident = sb("ident", [P, P])
        mask = sb("mask", [P, 2 * P])
        stats = sb("stats", [P, 2, GROUP, 6])
        moments = sb("moments", [P, 4, GROUP, 2])
        var_eps = sb("var_eps", [P, 4, GROUP])
        rstd = sb("rstd", [P, 4, GROUP])
        rstd_all = sb("rstd_all", [P, NT])
        mean_all = sb("mean_all", [P, NT])
        neg_half = sb("neg_half", [P, GROUP])
        xn_ring = sb("xn_ring", [P, 2, GROUP * D])
        xnT_ring = sb("xnT_ring", [P, 2, GROUP * P])
        taken = [0]

        def in_work(*shape):
            size = 1
            for n in shape:
                size *= n
            view = work[:, taken[0]:taken[0] + size]
            taken[0] += size
            if len(shape) == 2:
                return view.rearrange("p (a b) -> p a b", a=shape[0])
            return view

        first_key = sb("first_key", [P, E])
        best = sb("best", [P, NT])
        logits = in_work(NT, E)
        is_best = in_work(NT, E)
        chosen = in_work(E, NT)
        running = in_work(E, NT)
        zeros = sb("zeros", [P, E * NT])
        row_tot = sb("row_tot", [P, E])
        before = sb("before", [P, E])
        below = sb("below", [P, P])
        ones = sb("ones", [P, P])
        total = sb("total", [P, E])
        total_i = sb("total_i", [P, E], I32)
        run_i = sb("run_i", [P, E], I32)
        run = sb("run", [P, E])
        run_end = sb("run_end", [P, E])
        tiles_i = sb("tiles_i", [P, E], I32)
        tiles = sb("tiles", [P, E])
        tiles_end = sb("tiles_end", [P, E])
        base = sb("base", [P, E])
        cum_total = sb("cum_total", [P, E])
        pads_before = sb("pads_before", [P, E])
        offset = sb("offset", [P, E])
        pos_f = sb("pos_f", [P, NT])
        ids = sb("ids", [P, NT, 2], I32)
        pairs_i = sb("pairs_i", [P, E], I32)
        pairs = sb("pairs", [P, E])
        pairs_end = sb("pairs_end", [P, E])
        odd = sb("odd", [P, E])
        pair_no = sb("pair_no", [P, PAIRS + 2])
        pair_ge = in_work(PAIRS + 2, E)
        expert = sb("expert", [P, PAIRS + 2])
        skipped = sb("skipped", [P, PAIRS])
        experts_i = sb("experts_i", [P, PAIRS + 1], I32)
        pair_tile = sb("pair_tile", [P, 2, PAIRS])
        tile_ge = in_work(2 * PAIRS, E)
        tile_expert = sb("tile_expert", [P, 2, PAIRS])
        pair_row_i = sb("pair_row_i", [P, PAIRS], I32)
        void_i = sb("void_i", [P, PAIRS, 2], I32)
        pad_no = sb("pad_no", [P, NPAD])
        pad_ge = sb("pad_ge", [P, NPAD, E])
        pad_f = sb("pad_f", [P, NPAD])
        pad_i = sb("pad_i", [P, NPAD], I32)
        pad_row = sb("pad_row", [P, ROW])
        w_sum = sb("w_sum", [P, HC])
        w_top = sb("w_top", [P, 1])
        w_pow = sb("w_pow", [P, 1])
        w_recip = sb("w_recip", [P, 1])
        w_scale = sb("w_scale", [P, 1])
        h_scale = sb("h_scale", [P, 1])
        RB = 8
        y_sb = sb("y_sb", [P, 2, T])
        masked = in_work(2, 3 * P)
        neg_max = sb("neg_max", [P, 2, TB])
        probs = xnT_ring[:, :, 0:3 * P]
        inv_sum = sb("inv_sum", [P, 2, TB])
        probsT = sb("probsT", [P, 2, 3 * P])
        rows = x_all[:, 0:RB * TB * (ROW + 1)].rearrange("p (n r) -> p n r", r=ROW + 1)
        RC = 8
        tile_in = x_all[:, 0:RC * 2 * ROW].rearrange("p (s h r) -> p s h r", s=RC, h=2)
        xs_hi = sb("xs_hi", [P, 2, 2 * P], F16)
        xs_lo = sb("xs_lo", [P, 2, 2 * P], F16)
        out_ids = sb("out_ids", [P, RC, 2], I32)
        hidden = xnT_all[:, 0:4 * H].rearrange("p (s c t) -> p s c t", s=2, c=HC)
        tanh_y, y_gate, y_att = (
            xnT_all[:, 4 * H + i * 4 * D:4 * H + (i + 1) * 4 * D].rearrange("p (s t) -> p s t", s=2)
            for i in range(3))
        tile_out = xnT_all[:, 4 * H + 12 * D:4 * H + (12 + 2 * RC) * D].rearrange(
            "p (s h d) -> p s h d", s=RC, h=2)

        bank = [ctx.enter_context(nc.psum_tensor(f"bank{i}", [P, 512], F32)) for i in range(8)]

        w_loaded = sem("w_loaded")
        w1_loaded = sem("w1_loaded")
        w2_loaded = sem("w2_loaded")
        x_loaded = [sem(f"x_loaded{i}") for i in range(4)]
        const_step = sem("const_step")
        consts_ready = sem("consts_ready")
        wT_done = sem("wT_done")
        wT_copied = sem("wT_copied")
        a_done = sem("a_done")
        a_ready = sem("a_ready")
        stats_done = sem("stats_done")
        moments_ready = sem("moments_ready")
        eps_added = sem("eps_added")
        rstd_ready = sem("rstd_ready")
        xn_ready = sem("xn_ready")
        kept = sem("kept")
        xnT_done = sem("xnT_done")
        xnT_ready = sem("xnT_ready")
        xnT_stored = sem("xnT_stored")
        v_done = sem("v_done")
        v_ready = sem("v_ready")
        route_step = sem("route_step")
        counts_in = sem("counts_in")
        ones_set = sem("ones_set")
        counts_done = sem("counts_done")
        w_summed_up = sem("w_summed_up")
        places_ready = sem("places_ready")
        experts_ready = sem("experts_ready")
        pair_rows_ready = sem("pair_rows_ready")
        voids_ready = sem("voids_ready")
        pads_ready = sem("pads_ready")
        w_summed = sem("w_summed")
        scale_ready = sem("scale_ready")
        w_split = sem("w_split")
        hi_ready = sem("hi_ready")
        y_done = sem("y_done")
        y_ready = sem("y_ready")
        scores_done = sem("scores_done")
        masked_ready = sem("masked_ready")
        probs_ready = sem("probs_ready")
        probsT_done = sem("probsT_done")
        probsT_ready = sem("probsT_ready")
        att_done = sem("att_done")
        inv_ready = sem("inv_ready")
        row_x = [sem(f"row_x{i}") for i in range(RB)]
        row_xn = sem("row_xn")
        row_att = sem("row_att")
        row_sent = [sem(f"row_sent{i}") for i in range(RB)]
        pads_sent = sem("pads_sent")
        in_loaded = [sem(f"in_loaded{i}") for i in range(RC)]
        xsT_done = sem("xsT_done")
        xs_hi_ready = sem("xs_hi_ready")
        xs_lo_ready = sem("xs_lo_ready")
        up_done = sem("up_done")
        hidden_ready = sem("hidden_ready")
        down_done = sem("down_done")
        tanh_ready = sem("tanh_ready")
        gate_ready = sem("gate_ready")
        gated_ready = sem("gated_ready")
        out_ready = sem("out_ready")
        ids_ready = sem("ids_ready")
        out_sent = [sem(f"out_sent{i}") for i in range(RC)]

        def steady(eng, *waits):
            counts = [n if isinstance(n, int) else eng.to_reg(n) for _, n in waits]
            eng.wait_ge(consts_ready, 3)
            for (s, _), n in zip(waits, counts):
                eng.wait_ge(s, n)

        block = ctx.enter_context(nc.Block())

        @block.sync
        def _(sp):
            def load_x(g, turn, slot, least):
                if least >= 4:
                    sp.wait_ge(x_loaded[slot], 16 * turn)
                sp.dma_start(x_all[:, bass.ds(g * (GROUP * D), GROUP * D)],
                             x_tiles[:, bass.ds(g * GROUP, GROUP), :]).then_inc(x_loaded[slot], 16)

            def load_row_x(i, turn, slot, least):
                if least >= RB:
                    sp.wait_ge(row_sent[slot], 16 * TB * turn)
                sp.dma_start(rows[:, slot * TB:(slot + 1) * TB, 0:D],
                             x_tiles[:, bass.ds(i * TB, TB), :]).then_inc(row_x[slot], 16)

            def load_pair(k, turn, slot, least):
                if least >= RC:
                    sp.wait_ge(out_sent[slot], 32 * turn)
                row = nc.values_load(pair_row_i[0:1, bass.ds(k, 1)], engines=[sp.engine], min_val=0,
                                     max_val=(SLOTS - 2) * P,
                                     skip_runtime_bounds_check_because="at most the last pair's row")
                sp.dma_start(tile_in[:, slot, :, :],
                             buf[bass.ds(row, 2 * P), :].rearrange("(h p) r -> p h r", p=P)
                             ).then_inc(in_loaded[slot], 16)

            def load_rest(g, turn, slot, least):
                if least >= 2:
                    load_x(g, turn, slot, least)

            for g in range(2):
                load_x(g, 0, g, 0)
            sp.dma_start(wvg[:, 0:D], Wv).then_inc(w_loaded, 16)
            sp.dma_start(wvg[:, D:VW], Wg).then_inc(w_loaded, 16)
            sp.dma_start(wq_sb[:, :], Wq).then_inc(w_loaded, 16)
            sp.dma_start(wk_sb[:, :], Wk).then_inc(w_loaded, 16)
            sp.dma_start(bg_sb[:, :], bg_row.partition_broadcast(P)).then_inc(w_loaded, 16)
            pipeline(sp, NG, 4, 4, [(0, load_rest)])
            sp.dma_start(w1_all[:, :].rearrange("p (e h) -> p e h", e=E), w1_dram).then_inc(w1_loaded, 16)
            for c in range(HC):
                sp.dma_start(w2_sb[c][:, :].rearrange("p (e d) -> p e d", d=D),
                             w2_dram[:, :, c, :]).then_inc(w2_loaded, 16)
            sp.wait_ge(xn_ready, NG)
            pipeline(sp, B, RB, RB, [(0, load_row_x)])
            sp.wait_ge(pads_sent, 16 * NPAD)
            for slot in range(RB):
                sp.wait_ge(row_sent[slot], 16 * TB * (B // RB))
            sp.wait_ge(pair_rows_ready, 1)
            pipeline(sp, PAIRS, RC, RC, [(0, load_pair)])
            for slot in range(RC):
                sp.wait_ge(out_sent[slot], 32 * len(range(slot, PAIRS, RC)))

        @block.gpsimd
        def _(pool):
            pool.memset(neg_half[:, :], -0.5)
            pool.memset(ones[:, :], 1.0)
            pool.memset(ident[:, :], 0.0).then_inc(const_step, 1)
            pool.memset(mask[:, :], 0.0).then_inc(const_step, 1)
            pool.memset(below[:, :], 1.0).then_inc(const_step, 1)
            pool.wait_ge(const_step, 3)
            pool.affine_select(out=ident[:, :], in_=ident[:, :], compare_op=ALU.not_equal, fill=1.0,
                               base=0, pattern=[[-1, P]], channel_multiplier=1).then_inc(consts_ready, 1)
            pool.affine_select(out=mask[:, P:2 * P], in_=mask[:, P:2 * P], compare_op=ALU.is_ge, fill=-BIG,
                               base=0, pattern=[[-1, P]], channel_multiplier=1).then_inc(consts_ready, 1)
            pool.affine_select(out=below[:, :], in_=below[:, :], compare_op=ALU.is_gt, fill=0.0,
                               base=0, pattern=[[1, P]], channel_multiplier=-1).then_inc(consts_ready, 1)

            pool.iota(ids[:, :, 0], pattern=[[P, NT]], base=0, channel_multiplier=1).then_inc(consts_ready, 1)
            pool.memset(zeros[:, :], 0.0)
            pool.memset(pad_row[:, 0:3 * D], 0.0)
            pool.memset(pad_row[:, 3 * D:ROW].bitcast(I32), TOKENS)
            for e in range(E):
                pool.memset(first_key[:, e:e + 1], float(E - e))
            pool.iota(pad_no[:, :], pattern=[[P, NPAD]], base=0, channel_multiplier=1,
                      allow_small_or_imprecise_dtypes=True)
            pool.iota(pair_no[:, :], pattern=[[1, PAIRS + 2]], base=-1, channel_multiplier=0,
                      allow_small_or_imprecise_dtypes=True).then_inc(consts_ready, 1)

            def rstd_of(g, turn, slot, least):
                steady(pool, (moments_ready, g + 1))
                pool.tensor_scalar(var_eps[:, slot, :], moments[:, slot, :, 1], EPS, None,
                                   ALU.add).then_inc(eps_added, 1)
                pool.wait_ge(eps_added, g + 1)
                pool.tensor_tensor(rstd[:, slot, :], var_eps[:, slot, :], neg_half[:, :],
                                   ALU.pow).then_inc(rstd_ready, 1)
                pool.tensor_copy(mean_all[:, bass.ds(g * GROUP, GROUP)], moments[:, slot, :, 0])
                pool.wait_ge(rstd_ready, g + 1)
                pool.tensor_copy(rstd_all[:, bass.ds(g * GROUP, GROUP)], rstd[:, slot, :]).then_inc(kept, 1)

            pool.wait_ge(consts_ready, 3)
            pipeline(pool, NG, 4, 4, [(0, rstd_of)])
            pool.wait_ge(pads_ready, 1)
            for m in range(NPAD):
                pool.indirect_dma_start(out=buf[:, :], in_=pad_row[:, :], in_offset=None,
                                        out_offset=bass.IndirectOffsetOnAxis(ap=pad_i[:, m:m + 1], axis=0),
                                        bounds_check=SLOTS * P - 1,
                                        oob_is_err=False).then_inc(pads_sent, 16)

            def send(i, turn, slot, least):
                steady(pool, (row_x[slot], 16 * (turn + 1)), (row_xn, i + 1), (row_att, i + 1))
                for h in range(TB):
                    r = rows[:, slot * TB + h, :]
                    pool.indirect_dma_start(
                        out=buf[:, :], in_=r[:, 0:ROW], in_offset=None,
                        out_offset=bass.IndirectOffsetOnAxis(ap=r[:, ROW:ROW + 1].bitcast(I32), axis=0),
                        bounds_check=SLOTS * P - 1, oob_is_err=False).then_inc(row_sent[slot], 16)

            pipeline(pool, B, RB, RB, [(0, send)])

            def send_out(k, turn, slot, least):
                steady(pool, (out_ready, k + 1), (ids_ready, k + 1))
                for h in range(2):
                    pool.indirect_dma_start(
                        out=out_rows, in_=tile_out[:, slot, h, :], in_offset=None,
                        out_offset=bass.IndirectOffsetOnAxis(ap=out_ids[:, slot, h:h + 1], axis=0),
                        bounds_check=TOKENS - 1, oob_is_err=False).then_inc(out_sent[slot], 16)

            pipeline(pool, PAIRS, RC, RC, [(0, send_out)])

        @block.scalar
        def _(act):
            act.wait_ge(wT_done, 2)
            act.copy(wqT[:, :], bank[7][0:DQ, 0:P]).then_inc(wT_copied, 1)
            act.copy(wkT[:, :], bank[7][0:DQ, P:2 * P]).then_inc(wT_copied, 1)
            act.wait_ge(a_done, 1)
            act.copy(a_sb[:, :], bank[7][:, 2 * P:3 * P]).then_inc(a_ready, 1)

            def xnT_out(g, turn, slot, least):
                act.wait_ge(xnT_done, g + 1)
                if least >= 2:
                    act.wait_ge(v_done, g - 1)
                act.copy(xnT_ring[:, slot % 2, :], bank[slot % 2][:, :]).then_inc(xnT_ready, 1)
                act.copy(xnT_all[:, bass.ds(g * (GROUP * P), GROUP * P)],
                         bank[slot % 2][:, :]).then_inc(xnT_stored, 1)

            def v_out(g, turn, slot, least):
                act.wait_ge(v_done, g + 1)
                for h in range(2):
                    last = act.copy(v_all[:, bass.ds(g * (GROUP * VW) + h * 2 * VW, 2 * VW)],
                                    bank[2 + 2 * (slot % 2) + h][:, 0:2 * VW])
                last.then_inc(v_ready, 1)

            pipeline(act, NG, 4, 4, [(0, xnT_out), (1, v_out)])
            def y_out(i, turn, slot, least):
                act.wait_ge(y_done, i + 1)
                if least >= 2:
                    act.wait_ge(scores_done, i - 1)
                act.copy(y_sb[:, slot % 2, :],
                         bank[6 + slot % 2][:, 0:T]).then_inc(y_ready, 1)

            def sum_w1():
                act.wait_ge(w1_loaded, 16)
                for q in range(HC):
                    last = act.activation(w1_lo[q][:, :], w1_all[:, q * E * P:(q + 1) * E * P], ACT.Abs,
                                          accum_out=w_sum[:, q:q + 1])
                last.then_inc(w_summed, 1)

            def softmax(i, turn, slot, least):
                s = slot % 2
                if least == 0:
                    sum_w1()
                act.wait_ge(masked_ready, i + 1)
                if least >= 2:
                    act.wait_ge(probsT_done, i - 1)
                act.activation(probs[:, s, 0:P], masked[:, s, 0:P], ACT.Exp, bias=neg_max[:, s, 0:1],
                               scale=-1.0)
                act.activation(probs[:, s, P:3 * P], masked[:, s, P:3 * P], ACT.Exp, bias=neg_max[:, s, 1:2],
                               scale=-1.0).then_inc(probs_ready, 1)

            def probsT_out(i, turn, slot, least):
                s = slot % 2
                act.wait_ge(probsT_done, i + 1)
                if least >= 2:
                    act.wait_ge(att_done, i - 1)
                act.copy(probsT[:, s, :], bank[2 + s][:, 0:3 * P]).then_inc(probsT_ready, 1)
                if least == 0:
                    act.wait_ge(scale_ready, 1)
                act.activation(w1_hi[slot][:, bass.ds(turn * P, P)], w1_all[:, bass.ds(i * P, P)], ACT.Copy,
                               scale=w_scale[:, 0:1]).then_inc(hi_ready, 1)

            pipeline(act, B, HC, 8, [(0, y_out), (1, softmax), (2, probsT_out)])

            def gelu(k, turn, slot, least):
                s = slot % 2
                if least >= 2:
                    act.wait_ge(down_done, k - 1)
                for q in range(2):
                    act.wait_ge(up_done, 2 * k + q + 1)
                    act.activation(hidden[:, s, 2 * q:2 * q + 2, :].rearrange("p c t -> p (c t)"),
                                   bank[2 * s + q][:, :], ACT.Gelu_apprx_tanh,
                                   scale=h_scale[:, 0:1]).then_inc(hidden_ready, 1)

            def tanh(k, turn, slot, least):
                s = slot % 2
                act.wait_ge(down_done, k + 1)
                if least >= 2:
                    act.wait_ge(gate_ready, k - 1)
                act.activation(tanh_y[:, s, :], bank[4 + s][:, 0:2 * D], ACT.Tanh,
                               scale=0.5).then_inc(tanh_ready, 1)

            pipeline(act, PAIRS, 4, 4, [(0, gelu), (1, tanh)])

        @block.vector
        def _(dve):
            def stats_of(g, turn, slot, least):
                dve.wait_ge(x_loaded[slot], 16 * (turn + 1))
                if least >= 2:
                    dve.wait_ge(moments_ready, g - 1)
                for j in range(GROUP):
                    last = dve.bn_stats(stats[:, slot % 2, j, :],
                                        x_all[:, bass.ds(g * (GROUP * D) + j * D, D)])
                last.then_inc(stats_done, 1)

            def moments_of(g, turn, slot, least):
                if least >= 4:
                    dve.wait_ge(xn_ready, g - 3)
                    dve.wait_ge(kept, g - 3)
                steady(dve, (stats_done, g + 1))
                for j in range(GROUP):
                    last = dve.bn_aggr(moments[:, slot, j, :], stats[:, slot % 2, j, :])
                last.then_inc(moments_ready, 1)

            def normalise(g, turn, slot, least):
                dve.wait_ge(rstd_ready, g + 1)
                dve.wait_ge(moments_ready, g + 1)
                if least >= 2:
                    dve.wait_ge(xnT_done, g - 1)
                for j in range(GROUP):
                    last = dve.tensor_scalar(xn_ring[:, slot % 2, j * D:(j + 1) * D],
                                             x_all[:, bass.ds(g * (GROUP * D) + j * D, D)],
                                             moments[:, slot, j, 0:1], rstd[:, slot, j:j + 1],
                                             ALU.subtract, ALU.mult)
                last.then_inc(xn_ready, 1)

            dve.wait_ge(consts_ready, 3)
            pipeline(dve, NG, 4, 4, [(0, stats_of), (2, normalise), (0, moments_of)])

            def mask_max(i, turn, slot, least):
                s = slot % 2
                if least >= 2:
                    dve.wait_ge(probs_ready, i - 1)
                steady(dve, (scores_done, i + 1))
                dve.tensor_tensor_reduce(masked[:, s, 0:P], bank[s][:, 0:P], mask[:, P:2 * P],
                                         -(DQ ** -0.5), BIG, ALU.add, ALU.min, neg_max[:, s, 0:1])
                dve.tensor_tensor_reduce(masked[:, s, P:3 * P], bank[s][:, P:3 * P], mask[:, :],
                                         -(DQ ** -0.5), BIG, ALU.add, ALU.min,
                                         neg_max[:, s, 1:2]).then_inc(masked_ready, 1)

            steps = [0]

            def then(ins):
                steps[0] += 1
                ins.then_inc(route_step, 1)
                dve.wait_ge(route_step, steps[0])

            chosen_flat = chosen[:, :, :].rearrange("p e n -> p (e n)")
            running_flat = running[:, :, :].rearrange("p e n -> p (e n)")
            chosen_by_tile = chosen[:, :, :].rearrange("p e n -> p n e")
            v_by_tile = v_all[:, :].rearrange("p (n v) -> p n v", v=VW)
            dve.wait_ge(consts_ready, 5)
            dve.wait_ge(w_loaded, 80)
            for groups, n in ((NG - 3, slice(0, (NG - 3) * GROUP)), (NG, slice((NG - 3) * GROUP, NT))):
                shape = [P, n.stop - n.start, E]
                dve.wait_ge(v_ready, groups)
                then(dve.tensor_tensor(logits[:, n, :], v_by_tile[:, n, D:VW],
                                       bg_sb[:, None, :].broadcast_to(shape), ALU.add))
                then(dve.tensor_reduce(best[:, n], logits[:, n, :], AX.X, ALU.max))
                then(dve.tensor_tensor(is_best[:, n, :], logits[:, n, :], best[:, n, None].broadcast_to(shape),
                                       ALU.is_ge))
                then(dve.tensor_tensor(is_best[:, n, :], is_best[:, n, :],
                                       first_key[:, None, :].broadcast_to(shape), ALU.mult))
                then(dve.tensor_reduce(best[:, n], is_best[:, n, :], AX.X, ALU.max))
                then(dve.tensor_tensor(chosen_by_tile[:, n, :], first_key[:, None, :].broadcast_to(shape),
                                       best[:, n, None].broadcast_to(shape), ALU.is_equal))
            then(dve.tensor_tensor_scan(running_flat, zeros[:, :], chosen_flat, 0.0, ALU.add, ALU.add))
            dve.memset(before[:, 0:1], 0.0)
            then(dve.tensor_copy(before[:, 1:E], running[:, 0:E - 1, NT - 1]))
            dve.tensor_tensor(row_tot[:, :], running[:, :, NT - 1], before[:, :],
                              ALU.subtract).then_inc(counts_in, 1)
            dve.memset(v_by_tile[:, :, D:D + 1], 1.0).then_inc(ones_set, 1)
            mask_max(0, 0, 0, 0)
            dve.wait_ge(counts_done, 1)
            lower = bank[5][:, 0:E]
            dve.tensor_copy(total[:, :], bank[5][:, E:2 * E])
            then(dve.tensor_scalar(total_i[:, :], bank[5][:, E:2 * E], float(P - 1), None, ALU.add))
            dve.tensor_tensor_scan(cum_total[:, :], zeros[:, 0:E], total[:, :], 0.0, ALU.add, ALU.add)
            then(dve.tensor_scalar(run_i[:, :], total_i[:, :], ~(P - 1), None, ALU.bitwise_and))
            then(dve.tensor_copy(run[:, :], run_i[:, :]))
            then(dve.tensor_tensor_scan(run_end[:, :], zeros[:, 0:E], run[:, :], 0.0, ALU.add, ALU.add))
            dve.tensor_tensor(cum_total[:, :], cum_total[:, :], total[:, :], ALU.subtract)
            then(dve.tensor_tensor(base[:, :], run_end[:, :], run[:, :], ALU.subtract))
            then(dve.tensor_tensor(pads_before[:, :], base[:, :], cum_total[:, :], ALU.subtract))
            then(dve.tensor_tensor(pad_ge[:, :, :], pad_no[:, :, None].broadcast_to([P, NPAD, E]),
                                   pads_before[:, None, :].broadcast_to([P, NPAD, E]), ALU.is_ge))
            then(dve.tensor_tensor(pad_ge[:, :, :], pad_ge[:, :, :],
                                   total[:, None, :].broadcast_to([P, NPAD, E]), ALU.mult))
            then(dve.tensor_reduce(pad_f[:, :], pad_ge[:, :, :], AX.X, ALU.add))
            dve.tensor_tensor(pad_i[:, :], pad_f[:, :], pad_no[:, :], ALU.add).then_inc(pads_ready, 1)
            mask_max(1, 0, 1, 1)
            then(dve.tensor_tensor(running_flat, running_flat, chosen_flat, ALU.mult))
            then(dve.tensor_reduce(pos_f[:, :], running[:, :, :].rearrange("p e n -> p n e"), AX.X, ALU.add))
            then(dve.tensor_tensor(offset[:, :], base[:, :], before[:, :], ALU.subtract))
            then(dve.scalar_tensor_tensor(offset[:, :], offset[:, :], -1.0, lower, ALU.add, ALU.add))
            then(dve.tensor_tensor(is_best[:, :, :], chosen_by_tile,
                                   offset[:, None, :].broadcast_to([P, NT, E]), ALU.mult))
            then(dve.tensor_reduce(best[:, :], is_best[:, :, :], AX.X, ALU.add))
            dve.tensor_tensor(ids[:, :, 1], best[:, :], pos_f[:, :], ALU.add).then_inc(places_ready, 1)
            dve.wait_ge(w_summed_up, 1)
            then(dve.tensor_reduce(w_top[:, :], bank[4][:, 0:P], AX.X, ALU.max))
            then(dve.tensor_scalar(w_top[:, :], w_top[:, :], 1e-30, None, ALU.max))
            then(dve.tensor_scalar(w_pow[:, :].bitcast(I32), w_top[:, :].bitcast(I32), 0x7F800000, None,
                                   ALU.bitwise_and))
            then(dve.reciprocal(w_recip[:, :], w_pow[:, :]))
            then(dve.tensor_scalar(h_scale[:, :], w_pow[:, :], 1.0 / (W_TOP * XN_SCALE), None, ALU.mult))
            dve.tensor_scalar(w_scale[:, :], w_recip[:, :], W_TOP, None, ALU.mult).then_inc(scale_ready, 1)
            dve.wait_ge(scale_ready, 1)
            dve.wait_ge(places_ready, 1)

            def att_out(i, turn, slot, least):
                s = slot % 2
                if least >= RB:
                    dve.wait_ge(row_sent[slot], 16 * TB * turn)
                dve.wait_ge(row_x[slot], 16 * (turn + 1))
                r = rows[:, slot * TB:(slot + 1) * TB, :]
                for h in range(TB):
                    dve.tensor_scalar(r[:, h, D:2 * D], r[:, h, 0:D], mean_all[:, bass.ds(i * TB + h, 1)],
                                      rstd_all[:, bass.ds(i * TB + h, 1)], ALU.subtract, ALU.mult)
                dve.tensor_copy(r[:, :, 3 * D:3 * D + 2].bitcast(I32),
                                ids[:, bass.ds(i * TB, TB), :]).then_inc(row_xn, 1)
                dve.wait_ge(hi_ready, i + 1)
                c, e = slot % HC, turn * (RB // HC) + slot // HC
                dve.scalar_tensor_tensor(w1_lo[c][:, bass.ds(e * P, P)], w1_all[:, bass.ds(i * P, P)],
                                         w_scale[:, 0:1], w1_hi[c][:, bass.ds(e * P, P)], ALU.mult,
                                         ALU.subtract).then_inc(w_split, 1)
                dve.wait_ge(att_done, i + 1)
                att = bank[4 + s][:, 0:TB * (D + 1)].rearrange("p (n d) -> p n d", d=D + 1)
                if least >= 2:
                    dve.wait_ge(row_att, i - 1)
                dve.reciprocal(inv_sum[:, s, :], att[:, :, D]).then_inc(inv_ready, 1)
                dve.wait_ge(inv_ready, i + 1)
                dve.tensor_tensor(r[:, :, 2 * D:3 * D], att[:, :, 0:D],
                                  inv_sum[:, s, :, None].broadcast_to([P, TB, D]),
                                  ALU.mult).then_inc(row_att, 1)

            def mask_max_rest(i, turn, slot, least):
                if least >= 2:
                    mask_max(i, turn, slot, least)

            dve.wait_ge(kept, NG)
            pipeline(dve, B, RB, RB + 2, [(0, mask_max_rest), (2, att_out)])

            dve.tensor_scalar(tiles[:, :], run[:, :], 1.0 / P, None, ALU.mult)
            dve.tensor_scalar(tiles_end[:, :], run_end[:, :], 1.0 / P, None, ALU.mult)
            then(dve.tensor_scalar(tiles_i[:, :], total_i[:, :], 7, None, ALU.arith_shift_right))
            then(dve.tensor_scalar(pairs_i[:, :], tiles_i[:, :], 1, None, ALU.add))
            then(dve.tensor_scalar(pairs_i[:, :], pairs_i[:, :], 1, None, ALU.arith_shift_right))
            then(dve.tensor_copy(pairs[:, :], pairs_i[:, :]))
            then(dve.tensor_tensor_scan(pairs_end[:, :], zeros[:, 0:E], pairs[:, :], 0.0, ALU.add, ALU.add))
            then(dve.scalar_tensor_tensor(odd[:, :], pairs[:, :], 2.0, tiles[:, :], ALU.mult, ALU.subtract))
            then(dve.tensor_tensor(pair_ge[:, :, :], pair_no[:, :, None].broadcast_to([P, PAIRS + 2, E]),
                                   pairs_end[:, None, :].broadcast_to([P, PAIRS + 2, E]), ALU.is_ge))
            then(dve.tensor_reduce(expert[:, :], pair_ge[:, :, :], AX.X, ALU.add))
            then(dve.tensor_scalar(expert[:, :], expert[:, :], float(E - 1), None, ALU.min))
            dve.scalar_tensor_tensor(experts_i[:, :], expert[:, 1:PAIRS + 2], float(E),
                                     expert[:, 0:PAIRS + 1], ALU.mult, ALU.add).then_inc(experts_ready, 1)
            then(dve.tensor_tensor(pair_ge[:, :, :], pair_ge[:, :, :],
                                   odd[:, None, :].broadcast_to([P, PAIRS + 2, E]), ALU.mult))
            then(dve.tensor_reduce(skipped[:, :], pair_ge[:, 1:PAIRS + 1, :], AX.X, ALU.add))
            then(dve.scalar_tensor_tensor(pair_tile[:, 0, :], pair_no[:, 1:PAIRS + 1], 2.0, skipped[:, :],
                                          ALU.mult, ALU.subtract))
            then(dve.tensor_scalar(pair_tile[:, 1, :], pair_tile[:, 0, :], 1.0, None, ALU.add))
            then(dve.tensor_scalar(skipped[:, :], pair_tile[:, 0, :], float(SLOTS - 2), float(P), ALU.min,
                                   ALU.mult))
            dve.tensor_copy(pair_row_i[:, :], skipped[:, :]).then_inc(pair_rows_ready, 1)
            then(dve.tensor_tensor(
                tile_ge[:, :, :],
                pair_tile[:, :, :].rearrange("p h m -> p (h m)")[:, :, None].broadcast_to([P, 2 * PAIRS, E]),
                tiles_end[:, None, :].broadcast_to([P, 2 * PAIRS, E]), ALU.is_ge))
            then(dve.tensor_reduce(tile_expert[:, :, :].rearrange("p h m -> p (h m)"), tile_ge[:, :, :], AX.X,
                                   ALU.add))
            then(dve.tensor_tensor(tile_expert[:, :, :], tile_expert[:, :, :],
                                   expert[:, None, 1:PAIRS + 1].broadcast_to([P, 2, PAIRS]), ALU.is_gt))
            dve.tensor_scalar(void_i[:, :, :].rearrange("p m h -> p h m"), tile_expert[:, :, :],
                              float(VOID), None, ALU.mult).then_inc(voids_ready, 1)

            def split_xs(k, turn, slot, least):
                s = slot % 2
                dve.wait_ge(xsT_done, k + 1)
                if least >= 2:
                    dve.wait_ge(up_done, 2 * (k - 1))
                xsT = bank[6 + s][:, 0:2 * P]
                dve.tensor_scalar(xs_hi[:, s, :], xsT, XN_SCALE, None, ALU.mult).then_inc(xs_hi_ready, 1)
                if least >= RC:
                    dve.wait_ge(out_sent[slot], 32 * turn)
                dve.wait_ge(in_loaded[slot], 16 * (turn + 1))
                dve.tensor_tensor(out_ids[:, slot, :], tile_in[:, slot, :, 3 * D].bitcast(I32),
                                  void_i[:, bass.ds(k, 1), :].rearrange("p m h -> p (m h)"),
                                  ALU.bitwise_or).then_inc(ids_ready, 1)
                dve.wait_ge(xs_hi_ready, k + 1)
                dve.scalar_tensor_tensor(xs_lo[:, s, :], xsT, XN_SCALE, xs_hi[:, s, :], ALU.mult,
                                         ALU.subtract).then_inc(xs_lo_ready, 1)

            def combine(k, turn, slot, least):
                s = slot % 2
                dve.wait_ge(tanh_ready, k + 1)
                if least >= 2:
                    dve.wait_ge(gated_ready, k - 1)
                dve.scalar_tensor_tensor(y_gate[:, s, :], tanh_y[:, s, :], 1.0,
                                         bank[4 + s][:, 0:2 * D], ALU.add,
                                         ALU.mult).then_inc(gate_ready, 1)
                dve.wait_ge(gate_ready, k + 1)
                if least >= 2:
                    dve.wait_ge(out_ready, k - 1)
                halves = "p (h d) -> p h d"
                dve.tensor_tensor(y_att[:, s, :].rearrange(halves, h=2),
                                  y_gate[:, s, :].rearrange(halves, h=2), tile_in[:, slot, :, 2 * D:3 * D],
                                  ALU.mult).then_inc(gated_ready, 1)
                dve.wait_ge(gated_ready, k + 1)
                if least >= RC:
                    dve.wait_ge(out_sent[slot], 32 * turn)
                dve.scalar_tensor_tensor(tile_out[:, slot, :, :], y_att[:, s, :].rearrange(halves, h=2), 0.5,
                                         tile_in[:, slot, :, 0:D], ALU.mult,
                                         ALU.add).then_inc(out_ready, 1)

            dve.wait_ge(voids_ready, 1)
            pipeline(dve, PAIRS, RC, RC + 3, [(0, split_xs), (3, combine)])

        @block.tensor
        def _(pe):
            pe.wait_ge(consts_ready, 3)
            pe.wait_ge(w_loaded, 80)
            pe.transpose(bank[7][0:DQ, 0:P], wq_sb[:, :], ident[:, :]).then_inc(wT_done, 1)
            pe.transpose(bank[7][0:DQ, P:2 * P], wk_sb[:, :], ident[:, :]).then_inc(wT_done, 1)
            pe.wait_ge(wT_copied, 2)
            pe.matmul(bank[7][:, 2 * P:3 * P], wqT[:, :], wkT[:, :], start=True, stop=True).then_inc(a_done, 1)

            def xnT_of(g, turn, slot, least):
                pe.wait_ge(xn_ready, g + 1)
                if least >= 2:
                    pe.wait_ge(xnT_stored, g - 1)
                for j in range(GROUP):
                    last = pe.transpose(bank[slot % 2][:, j * P:(j + 1) * P],
                                        xn_ring[:, slot % 2, j * D:(j + 1) * D], ident[:, :])
                last.then_inc(xnT_done, 1)

            def v_of(g, turn, slot, least):
                pe.wait_ge(xnT_ready, g + 1)
                if least >= 2:
                    pe.wait_ge(v_ready, g - 1)
                for j in range(GROUP):
                    b = bank[2 + 2 * (slot % 2) + j // 2]
                    last = pe.matmul(b[:, (j % 2) * VW:(j % 2 + 1) * VW],
                                     xnT_ring[:, slot % 2, j * P:(j + 1) * P], wvg[:, :],
                                     start=True, stop=True)
                last.then_inc(v_done, 1)

            pipeline(pe, NG, 4, 4, [(0, xnT_of), (1, v_of)])

            pe.wait_ge(a_ready, 1)
            pe.wait_ge(v_ready, NG)
            pe.wait_ge(xnT_stored, NG)

            def route():
                pe.wait_ge(counts_in, 1)
                pe.matmul(bank[5][:, 0:E], below[:, :], row_tot[:, :], start=True, stop=True)
                pe.matmul(bank[5][:, E:2 * E], ones[:, :], row_tot[:, :], start=True,
                          stop=True).then_inc(counts_done, 1)
                pe.wait_ge(w_summed, 1)
                for q in range(HC):
                    last = pe.matmul(bank[4][:, 0:P], w_sum[:, q:q + 1].broadcast_to([P, P]), ident[:, :],
                                     start=(q == 0), stop=(q == HC - 1))
                last.then_inc(w_summed_up, 1)

            def y_of(i, turn, slot, least):
                if least >= 2:
                    pe.wait_ge(y_ready, i - 1)
                pe.matmul(bank[6 + slot % 2][:, 0:T], a_sb[:, :],
                          xnT_all[:, bass.ds(i * T, T)], start=True, stop=True).then_inc(y_done, 1)

            def scores_of(i, turn, slot, least):
                s = slot % 2
                pe.wait_ge(y_ready, i + 1)
                if least >= 2:
                    pe.wait_ge(masked_ready, i - 1)
                pe.matmul(bank[s][:, 0:P], y_sb[:, s, 0:P], xnT_all[:, bass.ds(i * T, P)],
                          start=True, stop=True)
                pe.matmul(bank[s][:, P:3 * P], y_sb[:, s, P:2 * P], xnT_all[:, bass.ds(i * T, T)],
                          start=True, stop=True).then_inc(scores_done, 1)

            def probsT_of(i, turn, slot, least):
                s = slot % 2
                if least == 0:
                    route()
                pe.wait_ge(probs_ready, i + 1)
                if least >= 2:
                    pe.wait_ge(probsT_ready, i - 1)
                for j in range(3):
                    last = pe.transpose(bank[2 + s][:, j * P:(j + 1) * P], probs[:, s, j * P:(j + 1) * P],
                                        ident[:, :])
                last.then_inc(probsT_done, 1)

            def att_of(i, turn, slot, least):
                s = slot % 2
                pe.wait_ge(probsT_ready, i + 1)
                if least == 0:
                    pe.wait_ge(ones_set, 1)
                    pe.wait_ge(scale_ready, 1)
                    pe.wait_ge(places_ready, 1)
                if least >= 2:
                    pe.wait_ge(row_att, i - 1)
                o = bank[4 + s]
                v0, v1 = (v_all[:, bass.ds(i * (TB * VW) + h * VW, D + 1)] for h in range(TB))
                pe.matmul(o[:, 0:D + 1], probsT[:, s, 0:P], v0, start=True, stop=True)
                pe.matmul(o[:, D + 1:2 * D + 2], probsT[:, s, P:2 * P], v0, start=True, stop=False)
                pe.matmul(o[:, D + 1:2 * D + 2], probsT[:, s, 2 * P:3 * P], v1, start=False,
                          stop=True).then_inc(att_done, 1)

            pipeline(pe, B, 4, 8, [(0, y_of), (1, scores_of), (2, probsT_of), (3, att_of)])

            pe.wait_ge(experts_ready, 1)
            pe.wait_ge(w_split, B)
            pe.wait_ge(w2_loaded, 16 * HC)

            def xsT_of(k, turn, slot, least):
                s = slot % 2
                pe.wait_ge(in_loaded[slot], 16 * (turn + 1))
                if least >= 2:
                    pe.wait_ge(xs_lo_ready, k - 1)
                for h in range(2):
                    last = pe.transpose(bank[6 + s][:, h * P:(h + 1) * P], tile_in[:, slot, h, D:2 * D],
                                        ident[:, :])
                last.then_inc(xsT_done, 1)

            experts = [None]

            def load_experts(k, turn, slot, least):
                experts[0] = nc.values_load(experts_i[0:1, bass.ds(k, 1)], engines=[pe.engine], min_val=0,
                                            max_val=E * E - 1,
                                            skip_runtime_bounds_check_because="each expert is at most E - 1")

            def up(k, turn, slot, least):
                own = pe.snap(experts[0] // E * P)
                s = slot % 2
                pe.wait_ge(xs_lo_ready, k + 1)
                if least >= 2:
                    pe.wait_ge(hidden_ready, 2 * (k - 1))
                for c in range(HC):
                    h = bank[2 * s + c // 2][:, c % 2 * 2 * P:(c % 2 + 1) * 2 * P]
                    hi = w1_hi[c][:, bass.ds(own, P)]
                    lo = w1_lo[c][:, bass.ds(own, P)]
                    pe.matmul(h, hi, xs_hi[:, s, :], start=True, stop=False)
                    pe.matmul(h, hi, xs_lo[:, s, :], start=False, stop=False)
                    last = pe.matmul(h, lo, xs_hi[:, s, :], start=False, stop=True)
                    if c % 2:
                        last.then_inc(up_done, 1)

            def down(k, turn, slot, least):
                if least == PAIRS - 1:
                    load_experts(k + 1, 0, 0, k + 1)
                own = pe.snap(experts[0] % E * P)
                s = slot % 2
                pe.wait_ge(hidden_ready, 2 * (k + 1))
                if least >= 2:
                    pe.wait_ge(gate_ready, k - 1)
                for h in range(2):
                    for c in range(HC):
                        last = pe.matmul(bank[4 + s][:, h * D:(h + 1) * D],
                                         hidden[:, s, c, h * P:(h + 1) * P],
                                         w2_sb[c][:, bass.ds(own, D)], start=(c == 0), stop=(c == HC - 1))
                last.then_inc(down_done, 1)

            pipeline(pe, PAIRS, RC, 4, [(1, load_experts), (0, xsT_of), (1, up), (2, down)])


_INS = ['L0_attn_X', 'L0_attn_Wq', 'L0_attn_Wk', 'L0_attn_Wv', 'L0_ffn_W1', 'L0_ffn_W2', 'L0_ffn_Wg', 'L0_ffn_bg']
_OUT = ((32, 256, 128), 'float32')


def kernel(**inputs):
    import numpy as _np
    import concourse.bacc as _bacc
    from concourse import mybir as _mybir
    from concourse.bass_utils import run_bass_kernel_spmd as _run

    nc = _bacc.Bacc("TRN2", target_bir_lowering=False, num_devices=1)
    arrays, args = {}, []
    for name in _INS:
        a = _np.ascontiguousarray(inputs[name])
        arrays[f"in_{name}_dram"] = a
        args.append(nc.dram_tensor(f"in_{name}_dram", a.shape, _mybir.dt.from_np(a.dtype), kind="ExternalInput").ap())
    shape, dtype = _OUT
    args.append(nc.dram_tensor("out_dram", shape, _mybir.dt.from_np(_np.dtype(dtype)), kind="ExternalOutput").ap())
    routed_block(nc, *args)
    r = _run(nc, [arrays], core_ids=[0])
    return r.results[0]["out_dram"]
```
